# Optimizing a Trainium2 kernel written in Bass

```python
import numpy as np
import jax
import jax.numpy as jnp

def _softmax(x, axis=-1):
    return jax.nn.softmax(x, axis=axis)

def _gelu(x):
    return jax.nn.gelu(x, approximate=True)

def _silu(x):
    return jax.nn.silu(x)

def _sigmoid(x):
    return jax.nn.sigmoid(x)

def _layernorm(x, axis=-1, eps=1e-05):
    m = jnp.mean(x, axis=axis, keepdims=True)
    v = jnp.var(x, axis=axis, keepdims=True)
    return (x - m) / jnp.sqrt(v + eps)

def _scatter_add(tgt, idx, src, axis=0):
    return tgt.at[idx].add(src)

def _segment_sum(src, seg, n):
    return jax.ops.segment_sum(src, seg, n)
kernel_name = 'mk_decoder_postln_d1_seqx_r8_c48b53'

def setup_inputs(seed: int=0):
    np.random.seed(seed)
    _w = jnp.asarray

    def _rec_inputs():
        import jax
        import jax.numpy as jnp
        _rk = jax.random.key(seed)
        x = -0.0003929 + 0.9999 * jax.random.normal(jax.random.fold_in(_rk, 1), (64, 64, 256), jnp.float32)
        _lenS = 64 - jax.random.randint(jax.random.fold_in(_rk, 7), (64,), 0, max(1, 64 // 4) + 1, jnp.int32)
        _lenS2 = 64 - jax.random.randint(jax.random.fold_in(_rk, 8), (64,), 0, max(1, 64 // 4) + 1, jnp.int32)
        _ctx_2048P = jax.random.normal(jax.random.fold_in(_rk, 11), (64, 16, 256), jnp.float32)
        _ctx_2048c = jax.random.dirichlet(jax.random.fold_in(_rk, 511), 0.3 * jnp.ones((16,), jnp.float32), (64, 64))
        _ctx_2048t = jnp.einsum('bsk,bkd->bsd', _ctx_2048c, _ctx_2048P)
        _ctx_2048t = _ctx_2048t * jax.lax.rsqrt(jnp.mean(jnp.square(_ctx_2048t)) + 1e-12) * 0.953939
        ctx_2048 = -1.39393e-06 + 0.999914 * (_ctx_2048t + 0.3 * jax.random.normal(jax.random.fold_in(_rk, 611), (64, 64, 256), jnp.float32))
        itok_BxS_0_1023 = jax.random.randint(jax.random.fold_in(_rk, 12), (64, 64), 0, 128, jnp.int32)
        return (x, ctx_2048, itok_BxS_0_1023)
    x, ctx_2048, itok_BxS_0_1023 = _rec_inputs()

    def _L0_attn_setup():
        import jax, jax.numpy as jnp
        import numpy as np
        import math
        N_HEAD = 16
        N_EMBD = 256
        HEAD_DIM = 128
        N_LAYER = 24
        EPS = 1e-05

        def _get_alibi_slopes(n_heads):

            def pow2(n):
                start = 2 ** (-2 ** (-(math.log2(n) - 3)))
                return [start * start ** i for i in range(n)]
            if math.log2(n_heads).is_integer():
                return pow2(n_heads)
            c = 2 ** math.floor(math.log2(n_heads))
            s = pow2(c)
            extra = _get_alibi_slopes(2 * c)
            return s + extra[0::2][:n_heads - c]
        ALIBI_SLOPES = jnp.asarray(np.array(_get_alibi_slopes(N_HEAD), dtype=np.float32))

        def rmsnorm(x, w, eps=EPS):
            xf = x.astype(jnp.float32)
            out = xf * jax.lax.rsqrt(jnp.mean(xf * xf, axis=-1, keepdims=True) + eps)
            return (out * w.astype(jnp.float32)).astype(x.dtype)
        key = jax.random.key(seed)
        ks = jax.random.split(key, 8)
        B, T, C, H, D = (2, 256, N_EMBD, N_HEAD, HEAD_DIM)
        sc = 1.0 / math.sqrt(C)
        proj_std = 0.5 / math.sqrt(C) / math.sqrt(N_LAYER)
        return {'x': jax.random.normal(ks[0], (B, T, C), jnp.float32), 'Wq': jax.random.normal(ks[1], (C, H * D), jnp.float32) * sc, 'Wk': jax.random.normal(ks[2], (C, H * D), jnp.float32) * sc, 'Wv': jax.random.normal(ks[3], (C, H * D), jnp.float32) * sc, 'Wproj': jax.random.normal(ks[4], (H * D, C), jnp.float32) * proj_std, 'q_rms_w': jnp.ones((D,), jnp.float32), 'k_rms_w': jnp.ones((D,), jnp.float32), 'subln_w': jnp.ones((D,), jnp.float32)}
    _L0_attn_all = _L0_attn_setup()
    _L0_attn_in = {k: v for k, v in _L0_attn_all.items() if k in ('Wq', 'Wk', 'Wv', 'Wproj', 'q_rms_w', 'k_rms_w', 'subln_w')}
    del _L0_attn_all

    def _L0_xattn_setup():
        import jax, jax.numpy as jnp
        import numpy as np
        B, Lq, Lk = (2, 512, 128)
        Q_DIM, KV_DIM = (256, 256)
        H, HD = (16, 128)
        KVC, QC, R = (64, 96, 64)
        LOOKBACK = 8
        NEG = -1e+30

        def _rope(x, L):
            half = x.shape[-1] // 2
            inv_freq = 1.0 / 10000.0 ** (jnp.arange(half, dtype=jnp.float32) / half)
            ang = jnp.arange(L, dtype=jnp.float32)[:, None] * inv_freq
            cos, sin = (jnp.cos(ang), jnp.sin(ang))
            x1, x2 = (x[..., :half], x[..., half:])
            return jnp.concatenate([x1 * cos - x2 * sin, x1 * sin + x2 * cos], axis=-1)
        key = jax.random.key(seed)
        ks = jax.random.split(key, 11)

        def w(k, shape, fan_in):
            return jax.random.normal(k, shape, jnp.float32) / np.sqrt(fan_in).astype(np.float32)
        return {'q': jax.random.normal(ks[0], (B, Lq, Q_DIM), jnp.float32), 'kv': jax.random.normal(ks[1], (B, Lk, KV_DIM), jnp.float32), 'seg_id': jnp.sort(jax.random.randint(ks[2], (B, Lq), 0, Lk), axis=-1), 'W_kvc': w(ks[3], (KV_DIM, KVC), KV_DIM), 'W_dq': w(ks[4], (Q_DIM, QC), Q_DIM), 'W_uq': w(ks[5], (QC, H * HD), QC), 'W_qr': w(ks[6], (QC, H * R), QC), 'W_uk': w(ks[7], (KVC, H * HD), KVC), 'W_kr': w(ks[8], (KVC, R), KVC), 'W_uv': w(ks[9], (KVC, H * HD), KVC), 'W_o': w(ks[10], (H * HD, Q_DIM), H * HD)}
    _L0_xattn_all = _L0_xattn_setup()
    _L0_xattn_in = {k: v for k, v in _L0_xattn_all.items() if k in ('W_kvc', 'W_dq', 'W_uq', 'W_qr', 'W_uk', 'W_kr', 'W_uv', 'W_o')}
    del _L0_xattn_all

    def _L0_ffn_setup():
        import jax, jax.numpy as jnp
        import numpy as np
        EPS = 1e-05

        def _quant_weight(w):
            scale = jnp.mean(jnp.abs(w)) + EPS
            wq = jnp.clip(jnp.round(w / scale), -1.0, 1.0) * scale
            return w + jax.lax.stop_gradient(wq - w)

        def _quant_act(x):
            scale = jnp.maximum(jnp.max(jnp.abs(x), axis=-1, keepdims=True), EPS) / 127.0
            xq = jnp.clip(jnp.round(x / scale), -128.0, 127.0) * scale
            return x + jax.lax.stop_gradient(xq - x)

        def bitlinear(x, w):
            return jnp.einsum('bsi,oi->bso', _quant_act(x), _quant_weight(w))
        key = jax.random.key(seed)
        k1, k2, k3, k4 = jax.random.split(key, 4)
        d_model, d_ff = (256, 1024)
        B, S = (4, 256)
        x = jax.random.normal(k1, (B, S, d_model), dtype=jnp.float32)
        w_gate = jax.random.normal(k2, (d_ff, d_model), dtype=jnp.float32) * 0.02
        w_up = jax.random.normal(k3, (d_ff, d_model), dtype=jnp.float32) * 0.02
        w_down = jax.random.normal(k4, (d_model, d_ff), dtype=jnp.float32) * 0.02
        return {'x': x, 'w_gate': w_gate, 'w_up': w_up, 'w_down': w_down}
    _L0_ffn_all = _L0_ffn_setup()
    _L0_ffn_in = {k: v for k, v in _L0_ffn_all.items() if k in ('w_gate', 'w_up', 'w_down')}
    del _L0_ffn_all
    return {'x': x, 'ctx_2048': ctx_2048, 'itok_BxS_0_1023': itok_BxS_0_1023, 'L0_attn_Wq': _L0_attn_in['Wq'], 'L0_attn_Wk': _L0_attn_in['Wk'], 'L0_attn_Wv': _L0_attn_in['Wv'], 'L0_attn_Wproj': _L0_attn_in['Wproj'], 'L0_attn_q_rms_w': _L0_attn_in['q_rms_w'], 'L0_attn_k_rms_w': _L0_attn_in['k_rms_w'], 'L0_attn_subln_w': _L0_attn_in['subln_w'], 'L0_xattn_W_kvc': _L0_xattn_in['W_kvc'], 'L0_xattn_W_dq': _L0_xattn_in['W_dq'], 'L0_xattn_W_uq': _L0_xattn_in['W_uq'], 'L0_xattn_W_qr': _L0_xattn_in['W_qr'], 'L0_xattn_W_uk': _L0_xattn_in['W_uk'], 'L0_xattn_W_kr': _L0_xattn_in['W_kr'], 'L0_xattn_W_uv': _L0_xattn_in['W_uv'], 'L0_xattn_W_o': _L0_xattn_in['W_o'], 'L0_ffn_w_gate': _L0_ffn_in['w_gate'], 'L0_ffn_w_up': _L0_ffn_in['w_up'], 'L0_ffn_w_down': _L0_ffn_in['w_down']}

def reference(x, ctx_2048, itok_BxS_0_1023, L0_attn_Wq, L0_attn_Wk, L0_attn_Wv, L0_attn_Wproj, L0_attn_q_rms_w, L0_attn_k_rms_w, L0_attn_subln_w, L0_xattn_W_kvc, L0_xattn_W_dq, L0_xattn_W_uq, L0_xattn_W_qr, L0_xattn_W_uk, L0_xattn_W_kr, L0_xattn_W_uv, L0_xattn_W_o, L0_ffn_w_gate, L0_ffn_w_up, L0_ffn_w_down):
    import jax
    import jax.numpy as jnp

    def _L0_attn_ref(x, Wq, Wk, Wv, Wproj, q_rms_w, k_rms_w, subln_w):
        import jax, jax.numpy as jnp
        import numpy as np
        import math
        N_HEAD = 16
        N_EMBD = 256
        HEAD_DIM = 128
        N_LAYER = 24
        EPS = 1e-05

        def _get_alibi_slopes(n_heads):

            def pow2(n):
                start = 2 ** (-2 ** (-(math.log2(n) - 3)))
                return [start * start ** i for i in range(n)]
            if math.log2(n_heads).is_integer():
                return pow2(n_heads)
            c = 2 ** math.floor(math.log2(n_heads))
            s = pow2(c)
            extra = _get_alibi_slopes(2 * c)
            return s + extra[0::2][:n_heads - c]
        ALIBI_SLOPES = jnp.asarray(np.array(_get_alibi_slopes(N_HEAD), dtype=np.float32))

        def rmsnorm(x, w, eps=EPS):
            xf = x.astype(jnp.float32)
            out = xf * jax.lax.rsqrt(jnp.mean(xf * xf, axis=-1, keepdims=True) + eps)
            return (out * w.astype(jnp.float32)).astype(x.dtype)
        B, T, C = x.shape
        H, D = (N_HEAD, HEAD_DIM)
        q = (x @ Wq).reshape(B, T, H, D)
        k = (x @ Wk).reshape(B, T, H, D)
        v = (x @ Wv).reshape(B, T, H, D)
        q = rmsnorm(q, q_rms_w)
        k = rmsnorm(k, k_rms_w)
        idx = jnp.arange(T)
        dist = jnp.maximum(idx[:, None] - idx[None, :], 0).astype(jnp.float32)
        bias = -dist[None, :, :] * ALIBI_SLOPES[:, None, None]
        causal = idx[:, None] >= idx[None, :]
        scale = 1.0 / math.sqrt(D)
        scores = jnp.einsum('bthd,bshd->bhts', q, k) * scale + bias[None]
        scores = jnp.where(causal[None, None], scores, -jnp.inf)
        attn = jax.nn.softmax(scores, axis=-1)
        y = jnp.einsum('bhts,bshd->bhtd', attn, v)
        y = rmsnorm(y, subln_w)
        y = y.transpose(0, 2, 1, 3).reshape(B, T, H * D)
        return y @ Wproj

    def _L0_xattn_ref(q, kv, seg_id, W_kvc, W_dq, W_uq, W_qr, W_uk, W_kr, W_uv, W_o):
        import jax, jax.numpy as jnp
        import numpy as np
        B, Lq, Lk = (2, 512, 128)
        Q_DIM, KV_DIM = (256, 256)
        H, HD = (16, 128)
        KVC, QC, R = (64, 96, 64)
        LOOKBACK = 8
        NEG = -1e+30

        def _rope(x, L):
            half = x.shape[-1] // 2
            inv_freq = 1.0 / 10000.0 ** (jnp.arange(half, dtype=jnp.float32) / half)
            ang = jnp.arange(L, dtype=jnp.float32)[:, None] * inv_freq
            cos, sin = (jnp.cos(ang), jnp.sin(ang))
            x1, x2 = (x[..., :half], x[..., half:])
            return jnp.concatenate([x1 * cos - x2 * sin, x1 * sin + x2 * cos], axis=-1)
        b, lq, _ = q.shape
        lk = kv.shape[1]
        kv_c = kv @ W_kvc
        q_c = q @ W_dq
        q_nope = (q_c @ W_uq).reshape(b, lq, H, HD).transpose(0, 2, 1, 3)
        q_rope = (q_c @ W_qr).reshape(b, lq, H, R).transpose(0, 2, 1, 3)
        k_nope = (kv_c @ W_uk).reshape(b, lk, H, HD)
        v = (kv_c @ W_uv).reshape(b, lk, H, HD)
        k_rope = kv_c @ W_kr
        q_rope = _rope(q_rope, lq)
        k_rope = _rope(k_rope, lk)
        scale = 1.0 / np.sqrt(HD + R).astype(np.float32)
        scores = (jnp.einsum('bhqd,bkhd->bhqk', q_nope, k_nope) + jnp.einsum('bhqr,bkr->bhqk', q_rope, k_rope)) * scale
        k_ids = jnp.arange(lk)[None, None, :]
        qs = seg_id[:, :, None]
        good = (k_ids <= qs) & (k_ids >= qs - LOOKBACK)
        scores = jnp.where(good[:, None, :, :], scores, NEG)
        attn = jax.nn.softmax(scores, axis=-1)
        out = jnp.einsum('bhqk,bkhd->bqhd', attn, v).reshape(b, lq, H * HD)
        return out @ W_o

    def _L0_ffn_ref(x, w_gate, w_up, w_down):
        import jax, jax.numpy as jnp
        import numpy as np
        EPS = 1e-05

        def _quant_weight(w):
            scale = jnp.mean(jnp.abs(w)) + EPS
            wq = jnp.clip(jnp.round(w / scale), -1.0, 1.0) * scale
            return w + jax.lax.stop_gradient(wq - w)

        def _quant_act(x):
            scale = jnp.maximum(jnp.max(jnp.abs(x), axis=-1, keepdims=True), EPS) / 127.0
            xq = jnp.clip(jnp.round(x / scale), -128.0, 127.0) * scale
            return x + jax.lax.stop_gradient(xq - x)

        def bitlinear(x, w):
            return jnp.einsum('bsi,oi->bso', _quant_act(x), _quant_weight(w))
        gate = jax.nn.sigmoid(bitlinear(x, w_gate))
        up = bitlinear(x, w_up)
        h = gate * up
        return bitlinear(h, w_down)
    x = _layernorm(x + _L0_attn_ref(x, L0_attn_Wq, L0_attn_Wk, L0_attn_Wv, L0_attn_Wproj, L0_attn_q_rms_w, L0_attn_k_rms_w, L0_attn_subln_w), axis=-1)
    x = _layernorm(x + _L0_xattn_ref(x, ctx_2048, itok_BxS_0_1023, L0_xattn_W_kvc, L0_xattn_W_dq, L0_xattn_W_uq, L0_xattn_W_qr, L0_xattn_W_uk, L0_xattn_W_kr, L0_xattn_W_uv, L0_xattn_W_o), axis=-1)
    x = _layernorm(x + _L0_ffn_ref(x, L0_ffn_w_gate, L0_ffn_w_up, L0_ffn_w_down), axis=-1)
    return x

_drawn_inputs = setup_inputs


def setup_inputs(seed=0):
    import zlib

    import numpy as np

    out = dict(_drawn_inputs(seed))
    spreads = {'L0_attn_q_rms_w': (1.0, 0.2),
     'L0_attn_k_rms_w': (1.0, 0.2),
     'L0_attn_subln_w': (1.0, 0.2)}
    factors = {'L0_ffn_w_gate': 8.0}
    for name, (base, spread) in spreads.items():
        noise = np.random.default_rng([zlib.crc32(name.encode()), seed]).standard_normal(out[name].shape)
        drawn = base * np.exp(spread * noise) if base else spread * noise
        out[name] = jnp.asarray(drawn.astype(out[name].dtype))
    for name, factor in factors.items():
        out[name] = (out[name] * factor).astype(out[name].dtype)
    return out
```

```python
import concourse.bass as bass
from concourse import mybir
from concourse.alu_op_type import AluOpType as ALU
from contextlib import ExitStack

F32 = mybir.dt.float32
BF16 = mybir.dt.bfloat16
I32 = mybir.dt.int32
ACT = mybir.ActivationFunctionType
AX = mybir.AxisListType.X

P = 128
B, T, C = 64, 64, 256
TOK = B * T
H, D = 16, 128
CC = C // P
TILE = 512
NT = TOK // TILE
PB = TILE // P
NB = TOK // P
BT = TILE // T
KVC, QC, R = 64, 96, 64
HP = H // 2
DFF = 1024
FC = DFF // P
EPS = 1e-5
NEG = -1e30
EXP_LN = "natural_log_exp_and_others"
LOOKBACK = 8
MAGIC = 12582912.0

PASSES = ((0, 0), (0, 1), (1, 0))


def wait(eng, sem, count):
    if not isinstance(count, int) or count > 0:
        eng.wait_ge(sem, count)


def high(tile, rows, lo, hi):
    return tile[rows, lo:hi].bitcast(BF16)[:, 1::2]


def slots(eng, slot, heads, inner=NT, lags=4):
    last = heads * inner
    for j in range(inner):
        slot(0, j, j, lambda lag: lag <= j)
    with eng.Fori(1, heads) as h:
        for j in range(inner):
            slot(h, j, h * inner + j, lambda lag: True)
    for j in range(lags - 1):
        slot(heads, j, last + j, lambda lag: lag > j)


def at(tile, i):
    return tile[:, i] if isinstance(i, int) else tile[:, bass.ds(i, 1)].squeeze(1)


def build(nc, a, out):
    ctx = ExitStack()
    with ctx:
        def sem(name):
            return ctx.enter_context(nc.semaphore(name))

        def sb(name, shape, dt, where=ctx):
            return where.enter_context(nc.sbuf_tensor(name, shape, dt))

        X = sb("X", [P, NB, C], F32)
        ident = sb("ident", [P, P], F32)
        eps_col = sb("eps_col", [P, 1], F32)
        with ExitStack() as part:
            self_attention(nc, a, X, ident, eps_col, sem, lambda n, s, d: sb(n, s, d, part), part)
        with ExitStack() as part:
            layer_norm(nc, X, eps_col, sem, lambda n, s, d: sb(n, s, d, part), "ln1")
        with ExitStack() as part:
            cross_attention(nc, a, X, ident, sem, lambda n, s, d: sb(n, s, d, part), part)
        with ExitStack() as part:
            layer_norm(nc, X, eps_col, sem, lambda n, s, d: sb(n, s, d, part), "ln2")
        with ExitStack() as part:
            feed_forward(nc, a, X, ident, sem, lambda n, s, d: sb(n, s, d, part), part)
        with ExitStack() as part:
            layer_norm(nc, X, eps_col, sem, lambda n, s, d: sb(n, s, d, part), "ln3", out)


def self_attention(nc, a, X, ident, eps_col, sem, sb, part):
    W = sb("W", [P, 2, 3, CC, H * D], BF16)
    xT = sb("xT", [P, 2, CC, TOK], BF16)
    Wp = sb("Wp", [P, 2, H, C], BF16)
    bias = sb("bias", [P, H, P], F32)
    qkw = sb("qkw", [P, 4], F32)
    ones = sb("ones", [P, P], BF16)

    with ExitStack() as own:
        stage = own.enter_context(nc.sbuf_tensor("stage", [P, 2, 2 * CC * TOK // 4], F32))
        s_const, s_x = sem("s_const"), sem("s_x")
        s_st = [sem("s_stage0"), sem("s_stage1")]
        s_hi, s_lo, s_scaled, s_w = sem("s_stage_hi"), sem("s_stage_lo"), sem("s_wproj_scaled"), sem("s_qkw")
        half = TOK // 2
        ROW = CC * H * D
        loads = []
        for i in range(2):
            loads.append((a["xT"].rearrange("(c p) t -> p c t", p=P)[:, :, i * half:(i + 1) * half],
                          [xT[:, k, :, i * half:(i + 1) * half] for k in range(2)], CC))
        for i, n in enumerate(("L0_attn_Wq", "L0_attn_Wk", "L0_attn_Wv")):
            loads.append((a[n].rearrange("(c p) n -> p c n", p=P), [W[:, k, i] for k in range(2)], CC))
        loads.append((a["L0_attn_Wproj"].rearrange("(h p) n -> p h n", p=P), [Wp[:, k] for k in range(2)], H))

        def staged(i):
            return stage[:, i % 2].rearrange("p (c n) -> p c n", c=loads[i][2])

        with nc.Block() as block:
            @block.sync
            def _(sp):
                for i, (src, _, _) in enumerate(loads):
                    if i >= 2:
                        sp.wait_ge(s_lo, i - 1)
                    sp.dma_start(staged(i), src).then_inc(s_st[i % 2], 16)
                    if i == 0:
                        for k, n in enumerate(("q_rms_w", "k_rms_w", "subln_w")):
                            sp.dma_start(qkw[:, k:k + 1], a["L0_attn_" + n].rearrange("(p o) -> p o", o=1)).then_inc(s_const, 16)
                        sp.dma_start(ident[:, :], a["ident"]).then_inc(s_const, 16)
                        sp.dma_start(bias[:, :, :], a["bias"].rearrange("p (h n) -> p h n", h=H)).then_inc(s_const, 16)
                sp.dma_start(X[:, :, :], a["x"].rearrange("(n p) c -> p n c", p=P)).then_inc(s_x, 16)
                sp.wait_ge(s_x, 16)

            @block.scalar
            def _(act):
                for i, (_, dst, _) in enumerate(loads):
                    act.wait_ge(s_st[i % 2], 16 * (i // 2 + 1))
                    if i == len(loads) - 1:
                        act.wait_ge(s_scaled, 1)
                    nc.scalar.activation(dst[0], staged(i), ACT.Copy).then_inc(s_hi, 1)

            @block.vector
            def _(dve):
                nc.vector.memset(ones[:, :], 1.0)
                nc.vector.memset(eps_col[:, :], EPS)
                dve.wait_ge(s_const, 5 * 16)
                nc.vector.scalar_tensor_tensor(qkw[:, 3:4], qkw[:, 0:1], D ** -0.5, qkw[:, 1:2],
                                               ALU.mult, ALU.mult).then_inc(s_w, 1)
                for i, (_, dst, _) in enumerate(loads):
                    dve.wait_ge(s_st[i % 2], 16 * (i // 2 + 1))
                    if i == len(loads) - 1:
                        nc.vector.tensor_scalar(stage[:, i % 2], stage[:, i % 2], qkw[:, 2:3], None,
                                                ALU.mult).then_inc(s_scaled, 1)
                    dve.wait_ge(s_hi, i + 1)
                    nc.vector.tensor_tensor(dst[1], staged(i), dst[0], ALU.subtract).then_inc(s_lo, 1)

    q_sq, k_sq, y_sq = sb("q_sq", [P, TILE], F32), sb("k_sq", [P, TILE], F32), sb("y_sq", [P, TILE], F32)
    q_sql, k_sql, y_sql = sb("q_sql", [P, TILE], BF16), sb("k_sql", [P, TILE], BF16), sb("y_sql", [P, TILE], BF16)
    rq, rk, ry = sb("rq", [P, TILE], F32), sb("rk", [P, TILE], F32), sb("ry", [P, TILE], F32)
    qn, kn, yn = sb("qn", [P, TILE], F32), sb("kn", [P, TILE], F32), sb("yn", [P, TILE], F32)
    ynl = sb("ynl", [P, TILE], BF16)
    VB = 4
    v = sb("v", [P, VB, PB, D], F32)
    scores = sb("scores", [P, PB, P], F32)
    probs = sb("probs", [P, PB, P], F32)
    probsT = sb("probsT", [P, TILE], F32)
    top, total, inv = sb("top", [P, PB], F32), sb("total", [P, PB], F32), sb("inv", [P, PB], F32)

    def ps(name, n=TILE):
        return part.enter_context(nc.psum_tensor(name, [P, n], F32))

    qP, kP, qssP, kssP, svP, pyP = ps("qP"), ps("kP"), ps("qssP"), ps("kssP"), ps("svP"), ps("pyP")
    projP = ps("projP", PB * C)
    yssP = projP[:, 0:TILE]

    s_q, s_k, s_v, s_s, s_pt, s_y, s_proj = (sem("a_" + n) for n in ("q", "k", "v", "s", "pt", "y", "proj"))
    s_qss, s_kss, s_yss = sem("a_qss"), sem("a_kss"), sem("a_yss")
    s_qsq, s_ksq, s_ysq = sem("a_qsq"), sem("a_ksq"), sem("a_ysq")
    s_qsql, s_ksql, s_ysql = sem("a_qsql"), sem("a_ksql"), sem("a_ysql")
    s_qln, s_kln, s_yln = sem("a_qln"), sem("a_kln"), sem("a_yln")
    s_rq, s_rk, s_ry = sem("a_rq"), sem("a_rk"), sem("a_ry")
    s_qn, s_kn, s_yn, s_ynl = sem("a_qn"), sem("a_kn"), sem("a_yn"), sem("a_ynl")
    s_ve, s_pte, s_bias, s_top, s_sub, s_exp = (sem("a_" + n) for n in ("ve", "pte", "bias", "top", "sub", "exp"))
    s_total, s_inv, s_norm, s_acc = sem("a_total"), sem("a_inv"), sem("a_norm"), sem("a_acc")

    with nc.Block() as block:
        @block.tensor
        def _(pe):
            def project(dst, w, h, tok):
                last = None
                for c in range(CC):
                    for i, (u, z) in enumerate(PASSES):
                        last = nc.tensor.matmul(dst[:, :], W[:, u, w, c, bass.ds(h * D, D)], xT[:, z, c, tok],
                                                start=(c == 0 and i == 0), stop=(c == CC - 1 and i == 2))
                return last

            def square_sum(dst, sq, low):
                nc.tensor.matmul(dst, ones[:, :], high(sq, slice(None), 0, TILE), start=True, stop=False)
                return nc.tensor.matmul(dst, ones[:, :], low[:, :], start=False, stop=True)

            def slot(h, j, n, has):
                tok = slice(j * TILE, (j + 1) * TILE)
                if has(0):
                    wait(pe, s_qn, n)
                    project(qP, 0, h, tok).then_inc(s_q, 1)
                    wait(pe, s_kn, n)
                    project(kP, 1, h, tok).then_inc(s_k, 1)
                if has(1):
                    wait(pe, s_qn, n)
                    wait(pe, s_kn, n)
                    wait(pe, s_ve, n)
                    for b in range(PB):
                        blk = slice(b * P, (b + 1) * P)
                        last = nc.tensor.matmul(svP[:, blk], qn[:, blk], kn[:, blk], start=True, stop=True)
                    last.then_inc(s_s, 1)
                if has(2):
                    wait(pe, s_norm, n - 1)
                    wait(pe, s_yn, n - 2)
                    for b in range(PB):
                        last = nc.tensor.transpose(pyP[:, b * P:(b + 1) * P], probs[:, b, :], ident[:, :])
                    last.then_inc(s_pt, 1)
                if has(3):
                    wait(pe, s_ynl, n - 2)
                    wait(pe, s_acc, n - 3)
                    wp = [at(Wp[:, z], h if j >= 3 else h - 1) for z in range(2)]
                    for b in range(PB):
                        for i, (u, z) in enumerate(PASSES):
                            y_part = high(yn, slice(None), b * P, (b + 1) * P) if u == 0 else ynl[:, b * P:(b + 1) * P]
                            last = nc.tensor.matmul(projP[:, b * C:(b + 1) * C], y_part, wp[z],
                                                    start=(i == 0), stop=(i == 2))
                    last.then_inc(s_proj, 1)
                if has(0):
                    wait(pe, s_qsql, n + 1)
                    square_sum(qssP[:, :], q_sq, q_sql).then_inc(s_qss, 1)
                    wait(pe, s_ksql, n + 1)
                    square_sum(kssP[:, :], k_sq, k_sql).then_inc(s_kss, 1)
                if has(2):
                    wait(pe, s_pte, n - 1)
                    vb = (j - 2) % VB
                    for b in range(PB):
                        last = nc.tensor.matmul(pyP[:, b * P:(b + 1) * P], v[:, vb, b, :], probsT[:, b * P:(b + 1) * P],
                                                start=True, stop=True)
                    last.then_inc(s_y, 1)
                if has(0):
                    wait(pe, s_bias, n)
                    for b in range(PB):
                        for c in range(CC):
                            for i, (u, z) in enumerate(PASSES):
                                last = nc.tensor.matmul(svP[:, b * D:(b + 1) * D],
                                                        xT[:, u, c, j * TILE + b * P:j * TILE + (b + 1) * P],
                                                        W[:, z, 2, c, bass.ds(h * D, D)],
                                                        start=(c == 0 and i == 0), stop=(c == CC - 1 and i == 2))
                    last.then_inc(s_v, 1)
                if has(2):
                    wait(pe, s_ysql, n - 1)
                    wait(pe, s_acc, n - 2)
                    square_sum(yssP, y_sq, y_sql).then_inc(s_yss, 1)

            slots(pe, slot, H)

        @block.scalar
        def _(act):
            def rsqrt_mean(r, ss, ready, count, s_ln, s_r):
                wait(act, ready, count)
                nc.scalar.activation(r[:, :], ss, ACT.Ln, bias=eps_col[:, :], scale=1.0 / D).then_inc(s_ln, 1)
                wait(act, s_ln, count)
                nc.scalar.activation(r[:, :], r[:, :], ACT.Exp, scale=-0.5).then_inc(s_r, 1)

            def slot(h, j, n, has):
                if has(3):
                    wait(act, s_yn, n - 3)
                    rsqrt_mean(ry, yssP, s_yss, n - 2, s_yln, s_ry)
                if has(0):
                    wait(act, s_q, n + 1)
                    nc.scalar.activation(q_sq[:, :], qP[:, :], ACT.Square).then_inc(s_qsq, 1)
                    wait(act, s_k, n + 1)
                    nc.scalar.activation(k_sq[:, :], kP[:, :], ACT.Square).then_inc(s_ksq, 1)
                if has(2):
                    wait(act, s_pt, n - 1)
                    nc.scalar.activation(probsT[:, :], pyP[:, :], ACT.Copy).then_inc(s_pte, 1)
                if has(0):
                    wait(act, s_qn, n)
                    rsqrt_mean(rq, qssP[:, :], s_qss, n + 1, s_qln, s_rq)
                if has(2):
                    wait(act, s_y, n - 1)
                    nc.scalar.activation(y_sq[:, :], pyP[:, :], ACT.Square).then_inc(s_ysq, 1)
                if has(0):
                    wait(act, s_kn, n)
                    rsqrt_mean(rk, kssP[:, :], s_kss, n + 1, s_kln, s_rk)
                if has(1):
                    wait(act, s_sub, n)
                    wait(act, s_pt, n - 1)
                    nc.scalar.activation(probs[:, :, :], scores[:, :, :], ACT.Exp).then_inc(s_exp, 1)

            nc.scalar.preload_act_table_set(EXP_LN)
            slots(act, slot, H)

        @block.vector
        def _(dve):
            def slot(h, j, n, has):
                if has(1):
                    wait(dve, s_rk, n)
                    nc.vector.scalar_tensor_tensor(kn[:, :], kP[:, :], qkw[:, 3:4], rk[:, :], ALU.mult, ALU.mult).then_inc(s_kn, 1)
                    wait(dve, s_v, n)
                    nc.vector.tensor_copy(v[:, (j - 1) % VB], svP[:, :].rearrange("p (b d) -> p b d", b=PB)).then_inc(s_ve, 1)
                if has(2):
                    wait(dve, s_exp, n - 1)
                    nc.vector.tensor_reduce(total[:, :], probs[:, :, :], AX, ALU.add).then_inc(s_total, 1)
                    wait(dve, s_total, n - 1)
                    nc.vector.reciprocal(inv[:, :], total[:, :]).then_inc(s_inv, 1)
                if has(3):
                    wait(dve, s_ry, n - 2)
                    nc.vector.tensor_tensor(yn[:, :], pyP[:, :], ry[:, :], ALU.mult).then_inc(s_yn, 1)
                if has(0):
                    wait(dve, s_ksq, n + 1)
                    wait(dve, s_kss, n)
                    nc.vector.tensor_tensor(k_sql[:, :], k_sq[:, :], high(k_sq, slice(None), 0, TILE), ALU.subtract).then_inc(s_ksql, 1)
                if has(1):
                    row = at(bias, h if j >= 1 else h - 1)
                    wait(dve, s_s, n)
                    nc.vector.tensor_tensor(scores[:, :, :], svP[:, :].rearrange("p (b s) -> p b s", b=PB),
                                            row.unsqueeze(1).to_broadcast([P, PB, P]), ALU.add).then_inc(s_bias, 1)
                    wait(dve, s_bias, n)
                    nc.vector.tensor_reduce(top[:, :], scores[:, :, :], AX, ALU.max).then_inc(s_top, 1)
                if has(3):
                    jj = (j - 3) % NT
                    acc = X[:, jj * PB:(jj + 1) * PB, :]
                    wait(dve, s_proj, n - 2)
                    wait(dve, s_acc, n - 3)
                    nc.vector.tensor_tensor(acc, projP[:, :].rearrange("p (b c) -> p b c", b=PB), acc, ALU.add).then_inc(s_acc, 1)
                if has(0):
                    wait(dve, s_rq, n + 1)
                    nc.vector.tensor_tensor(qn[:, :], qP[:, :], rq[:, :], ALU.mult).then_inc(s_qn, 1)

            slots(dve, slot, H)

        @block.gpsimd
        def _(pool):
            def slot(h, j, n, has):
                if has(2):
                    wait(pool, s_inv, n - 1)
                    nc.gpsimd.tensor_tensor(probs[:, :, :], probs[:, :, :], inv[:, :].unsqueeze(2).to_broadcast([P, PB, P]), ALU.mult).then_inc(s_norm, 1)
                if has(3):
                    wait(pool, s_yn, n - 2)
                    wait(pool, s_proj, n - 3)
                    nc.gpsimd.tensor_tensor(ynl[:, :], yn[:, :], high(yn, slice(None), 0, TILE), ALU.subtract).then_inc(s_ynl, 1)
                if has(0):
                    wait(pool, s_qsq, n + 1)
                    wait(pool, s_qss, n)
                    nc.gpsimd.tensor_tensor(q_sql[:, :], q_sq[:, :], high(q_sq, slice(None), 0, TILE), ALU.subtract).then_inc(s_qsql, 1)
                if has(1):
                    wait(pool, s_top, n)
                    nc.gpsimd.tensor_tensor(scores[:, :, :], scores[:, :, :], top[:, :].unsqueeze(2).to_broadcast([P, PB, P]), ALU.subtract).then_inc(s_sub, 1)
                if has(2):
                    wait(pool, s_ysq, n - 1)
                    wait(pool, s_yss, n - 2)
                    nc.gpsimd.tensor_tensor(y_sql[:, :], y_sq[:, :], high(y_sq, slice(None), 0, TILE), ALU.subtract).then_inc(s_ysql, 1)

            slots(pool, slot, H)


def layer_norm(nc, X, eps_col, sem, sb, tag, out=None):
    stats = sb(tag + "_stats", [P, NB, 6], F32)
    mean, var = sb(tag + "_mean", [P, NB], F32), sb(tag + "_var", [P, NB], F32)
    gap, rstd, shift = sb(tag + "_gap", [P, NB], F32), sb(tag + "_rstd", [P, NB], F32), sb(tag + "_shift", [P, NB], F32)
    s_stats, s_small, s_ln, s_rstd, s_shift = (sem(f"{tag}_{n}") for n in ("stats", "small", "ln", "rstd", "shift"))
    s_dve, s_act, s_out = sem(tag + "_dve"), sem(tag + "_act"), sem(tag + "_out")
    own = PB // 2
    with nc.Block() as block:
        @block.vector
        def _(dve):
            with dve.Fori(0, NT) as j:
                for b in range(PB):
                    nc.vector.bn_stats(at(stats, j * PB + b), at(X, j * PB + b)).then_inc(s_stats, 1)
            dve.wait_ge(s_stats, NB)
            nc.vector.tensor_tensor(mean[:, :], stats[:, :, 1], stats[:, :, 4], ALU.add).then_inc(s_small, 1)
            nc.vector.tensor_tensor(gap[:, :], stats[:, :, 1], stats[:, :, 4], ALU.subtract).then_inc(s_small, 1)
            nc.vector.tensor_tensor(var[:, :], stats[:, :, 2], stats[:, :, 5], ALU.add).then_inc(s_small, 1)
            dve.wait_ge(s_small, 3)
            nc.vector.tensor_scalar(mean[:, :], mean[:, :], 0.5, None, ALU.mult).then_inc(s_small, 1)
            nc.vector.scalar_tensor_tensor(gap[:, :], gap[:, :], 0.25, gap[:, :], ALU.mult, ALU.mult).then_inc(s_small, 1)
            dve.wait_ge(s_small, 5)
            nc.vector.scalar_tensor_tensor(var[:, :], var[:, :], 1.0 / C, gap[:, :], ALU.mult, ALU.add).then_inc(s_small, 1)
            dve.wait_ge(s_rstd, 1)
            nc.vector.scalar_tensor_tensor(shift[:, :], mean[:, :], -1.0, rstd[:, :], ALU.mult, ALU.mult).then_inc(s_shift, 1)
            with dve.Fori(0, NT) as j:
                for b in range(own):
                    x = at(X, j * PB + b)
                    last = nc.vector.tensor_scalar(x, x, mean[:, bass.ds(j * PB + b, 1)], rstd[:, bass.ds(j * PB + b, 1)],
                                                   ALU.subtract, ALU.mult)
                last.then_inc(s_dve, 1)

        @block.scalar
        def _(act):
            nc.scalar.preload_act_table_set(EXP_LN)
            act.wait_ge(s_small, 6)
            nc.scalar.activation(rstd[:, :], var[:, :], ACT.Ln, bias=eps_col[:, :]).then_inc(s_ln, 1)
            act.wait_ge(s_ln, 1)
            nc.scalar.activation(rstd[:, :], rstd[:, :], ACT.Exp, scale=-0.5).then_inc(s_rstd, 1)
            act.wait_ge(s_shift, 1)
            with act.Fori(0, NT) as j:
                for b in range(own, PB):
                    x = at(X, j * PB + b)
                    last = nc.scalar.activation(x, x, ACT.Identity, bias=shift[:, bass.ds(j * PB + b, 1)],
                                                scale=rstd[:, bass.ds(j * PB + b, 1)])
                last.then_inc(s_act, 1)

        if out is not None:
            @block.sync
            def _(sp):
                dst = out.rearrange("(n p) c -> p n c", p=P)
                with sp.Fori(0, NT) as j:
                    sp.wait_ge(s_dve, j + 1)
                    sp.wait_ge(s_act, j + 1)
                    sp.dma_start(dst[:, bass.ds(j * PB, PB), :], X[:, bass.ds(j * PB, PB), :]).then_inc(s_out, 16)
                sp.wait_ge(s_out, 16 * NT)


def cross_attention(nc, a, X, ident, sem, sb, part):
    qc = sb("qc", [P, 2, TOK], BF16)
    kh = sb("kh", [P, 2, TOK], BF16)
    KV = sb("KV", [P, NB, P], F32)
    WQ = sb("WQ", [P, 2, HP, 3, P], BF16)
    WB = sb("WB", [P, 2, HP, C], BF16)
    mask = sb("mask", [P, B, T], F32)
    tabs = sb("tabs", [P, 4, T], F32)
    s_setup = sem("x_setup")

    with ExitStack() as own:
        def tmp(name, shape, dt=F32):
            return own.enter_context(nc.sbuf_tensor(name, shape, dt))

        def ps(name, n=TILE):
            return own.enter_context(nc.psum_tensor(name, [P, n], F32))

        ctxf, ctxT = tmp("ctxf", [P, CC, TILE]), tmp("ctxT", [P, 2, CC, TILE], BF16)
        x1T = tmp("x1T", [P, 2, CC, TILE], BF16)
        dqf, dq = tmp("dqf", [P, CC, QC]), tmp("dq", [P, 2, CC, QC], BF16)
        kvf, kvw = tmp("kvf", [P, CC, KVC]), tmp("kvw", [P, 2, CC, KVC], BF16)
        wkr = tmp("wkr", [KVC, 2 * R])
        uqT, ukT, uvT = tmp("uqT", [P, H, QC]), tmp("ukT", [P, H, KVC]), tmp("uvT", [P, H, KVC])
        wo = tmp("wo", [P, H, C])
        qr, qrs = tmp("qr", [QC, H * R]), tmp("qrs", [QC, H * R])
        kf, ksw = tmp("kf", [P, TILE]), tmp("ksw", [P, TILE])
        seg, segf, keys = tmp("seg", [P, B], I32), tmp("segf", [P, B]), tmp("keys", [P, T])
        s_ld, s_ctx = sem("x_loads"), sem("x_ctx")
        n_loads = 16

        with ExitStack() as fold:
            AP_ = fold.enter_context(nc.psum_tensor("foldA", [P, H * KVC], F32))
            BP_ = fold.enter_context(nc.psum_tensor("foldB", [P, HP * C], F32))
            s_A, s_B, s_whi, s_wlo, s_z, s_m = (sem("x_" + n) for n in ("A", "B", "whi", "wlo", "zero", "mask"))
            foldA = AP_[0:QC, :].rearrange("p (g i k) -> p g i k", g=HP, i=2)
            foldB = BP_[:, :].rearrange("p (g c) -> p g c", g=HP)
            qr_v = qr[:, :].rearrange("p (g i k) -> p g i k", g=HP, i=2)
            qrs_v = qrs[:, :].rearrange("p (g i k) -> p g i k", g=HP, i=2)
            splits = [(dqf[:, :, :], lambda k: dq[:, k]), (kvf[:, :, :], lambda k: kvw[:, k]),
                      (qr_v, lambda k: WQ[0:QC, k, :, 0:2, KVC:P]),
                      (qrs_v[:, :, 1], lambda k: WQ[0:QC, k, :, 2, 0:R]),
                      (qrs_v[:, :, 0], lambda k: WQ[0:QC, k, :, 2, R:P]),
                      (foldA, lambda k: WQ[0:QC, k, :, 0:2, 0:KVC]),
                      (foldB, lambda k: WB[:, k])]
            with nc.Block() as block:
                @block.sync
                def _(sp):
                    loads = [(dqf[:, :, :], a["L0_xattn_W_dq"].rearrange("(c p) n -> p c n", p=P)),
                             (kvf[:, :, :], a["L0_xattn_W_kvc"].rearrange("(c p) n -> p c n", p=P)),
                             (wkr[:, :], a["wkr"]),
                             (uqT[:, :, :], a["uqT"].rearrange("(h p) n -> p h n", p=P)),
                             (ukT[:, :, :], a["ukT"].rearrange("(h p) n -> p h n", p=P)),
                             (uvT[:, :, :], a["uvT"].rearrange("(h p) n -> p h n", p=P)),
                             (wo[:, :, :], a["L0_xattn_W_o"].rearrange("(h p) n -> p h n", p=P)),
                             (qr[:, :], a["L0_xattn_W_qr"]), (qrs[:, :], a["qrs"]),
                             (tabs[:, :, :], a["rope"].rearrange("p (k t) -> p k t", k=4)),
                             (keys[:, :], a["keys"]),
                             (seg[0:T, :], a["segT"]), (seg[T:P, :], a["segT"])]
                    for dst, src in loads:
                        sp.dma_start(dst, src).then_inc(s_ld, 16)
                    assert len(loads) == 13

                @block.gpsimd
                def _(pool):
                    nc.gpsimd.memset(WQ[:, :, :, :, :], 0.0).then_inc(s_z, 1)
                    nc.gpsimd.memset(qc[:, :, :], 0.0)
                    nc.gpsimd.memset(KV[:, :, :], 0.0)

                @block.tensor
                def _(pe):
                    pe.wait_ge(s_ld, 13 * 16)
                    for h in range(H):
                        last = nc.tensor.matmul(AP_[0:QC, h * KVC:(h + 1) * KVC], uqT[:, h, :], ukT[:, h, :], start=True, stop=True)
                    last.then_inc(s_A, 1)
                    for h in range(H):
                        o = KVC * (h % 2)
                        last = nc.tensor.matmul(BP_[o:o + KVC, (h // 2) * C:(h // 2 + 1) * C], uvT[:, h, :], wo[:, h, :], start=True, stop=True)
                    last.then_inc(s_B, 1)

                @block.scalar
                def _(act):
                    act.wait_ge(s_ld, 13 * 16)
                    act.wait_ge(s_z, 1)
                    for i, (src, dst) in enumerate(splits):
                        if src is foldA:
                            act.wait_ge(s_A, 1)
                        if src is foldB:
                            act.wait_ge(s_B, 1)
                        nc.scalar.activation(dst(0), src, ACT.Copy).then_inc(s_whi, 1)

                @block.vector
                def _(dve):
                    dve.wait_ge(s_ld, 13 * 16)
                    nc.vector.tensor_copy(segf[:, :], seg[:, :]).then_inc(s_m, 1)
                    dve.wait_ge(s_m, 1)
                    nc.vector.tensor_tensor(mask[:, :, :], segf[:, :].unsqueeze(2).to_broadcast([P, B, T]),
                                            keys[:, :].unsqueeze(1).to_broadcast([P, B, T]), ALU.subtract).then_inc(s_m, 1)
                    dve.wait_ge(s_m, 2)
                    nc.vector.tensor_tensor(mask[:, :, :], mask[:, :, :], mask[:, :, :], ALU.mult).then_inc(s_m, 1)
                    dve.wait_ge(s_m, 3)
                    nc.vector.tensor_scalar(mask[:, :, :], mask[:, :, :], (LOOKBACK / 2) ** 2, NEG, ALU.is_gt, ALU.mult).then_inc(s_m, 1)
                    for i, (src, dst) in enumerate(splits):
                        dve.wait_ge(s_whi, i + 1)
                        nc.vector.tensor_tensor(dst(1), src, dst(0), ALU.subtract).then_inc(s_wlo, 1)

        kvP, krP, ksP, tkP, qcP = ps("kvP"), ps("krP"), ps("ksP"), ps("tkP"), ps("qcP")
        xtP = ps("xtP", CC * TILE)
        n_ = ("chi", "clo", "kv", "kf", "kr", "krr", "kss", "kf2", "khi", "klo", "tk", "tke", "xt", "xhi", "xlo", "qc", "qhi", "qlo", "krs")
        t_ = {n: sem("xp_" + n) for n in n_}
        with nc.Block() as block:
            @block.sync
            def _(sp):
                src = a["ctxT"].rearrange("(c p) t -> p c t", p=P)
                for j in range(NT):
                    if j:
                        sp.wait_ge(t_["clo"], j)
                    sp.dma_start(ctxf[:, :, :], src[:, :, j * TILE:(j + 1) * TILE]).then_inc(s_ctx, 16)

            @block.tensor
            def _(pe):
                for j in range(NT):
                    for c in range(CC):
                        for b in range(PB):
                            if c == 0 and b == 0 and j:
                                pe.wait_ge(t_["xlo"], j)
                            last = nc.tensor.transpose(xtP[:, c * TILE + b * P:c * TILE + (b + 1) * P],
                                                       X[:, j * PB + b, c * P:(c + 1) * P], ident[:, :])
                    last.then_inc(t_["xt"], 1)
                    pe.wait_ge(t_["clo"], j + 1)
                    if j:
                        pe.wait_ge(t_["kf"], j)
                    for c in range(CC):
                        for i, (u, z) in enumerate(PASSES):
                            last = nc.tensor.matmul(kvP[0:KVC, :], kvw[:, u, c, :], ctxT[:, z, c, :],
                                                    start=(c == 0 and i == 0), stop=(c == CC - 1 and i == 2))
                    last.then_inc(t_["kv"], 1)
                    if j:
                        pe.wait_ge(t_["tke"], j)
                    for b in range(PB):
                        for c in range(CC):
                            for i, (u, z) in enumerate(PASSES):
                                last = nc.tensor.matmul(tkP[:, b * KVC:(b + 1) * KVC], ctxT[:, u, c, b * P:(b + 1) * P], kvw[:, z, c, :],
                                                        start=(c == 0 and i == 0), stop=(c == CC - 1 and i == 2))
                    last.then_inc(t_["tk"], 1)
                    pe.wait_ge(t_["xlo"], j + 1)
                    if j:
                        pe.wait_ge(t_["qlo"], j)
                    for c in range(CC):
                        for i, (u, z) in enumerate(PASSES):
                            last = nc.tensor.matmul(qcP[0:QC, :], dq[:, u, c, :], x1T[:, z, c, :],
                                                    start=(c == 0 and i == 0), stop=(c == CC - 1 and i == 2))
                    last.then_inc(t_["qc"], 1)
                    pe.wait_ge(t_["kf"], j + 1)
                    if j:
                        pe.wait_ge(t_["kss"], j)
                    nc.tensor.matmul(krP[R:P, :], wkr[:, 0:R], kf[0:KVC, :], start=True, stop=True)
                    nc.tensor.matmul(ksP[R:P, :], wkr[:, R:2 * R], kf[0:KVC, :], start=True, stop=True).then_inc(t_["kr"], 1)

            @block.scalar
            def _(act):
                for j in range(NT):
                    tok = slice(j * TILE, (j + 1) * TILE)
                    act.wait_ge(s_ctx, 16 * (j + 1))
                    if j:
                        act.wait_ge(t_["tk"], j)
                    nc.scalar.activation(ctxT[:, 0], ctxf[:, :, :], ACT.Copy).then_inc(t_["chi"], 1)
                    act.wait_ge(t_["xt"], j + 1)
                    if j:
                        act.wait_ge(t_["qc"], j)
                    nc.scalar.activation(x1T[:, 0], xtP[:, :].rearrange("p (c t) -> p c t", c=CC), ACT.Copy).then_inc(t_["xhi"], 1)
                    act.wait_ge(t_["kv"], j + 1)
                    if j:
                        act.wait_ge(t_["klo"], j)
                    nc.scalar.activation(kf[0:KVC, :], kvP[0:KVC, :], ACT.Copy).then_inc(t_["kf"], 1)
                    act.wait_ge(t_["tk"], j + 1)
                    tk = tkP[:, 0:PB * KVC].rearrange("p (b k) -> p b k", b=PB)
                    nc.scalar.activation(KV[0:T, j * PB:(j + 1) * PB, 0:KVC], tk[0:T], ACT.Copy)
                    nc.scalar.activation(KV[T:P, j * PB:(j + 1) * PB, KVC:P], tk[T:P], ACT.Copy).then_inc(t_["tke"], 1)
                    act.wait_ge(t_["qc"], j + 1)
                    nc.scalar.activation(qc[0:QC, 0, tok], qcP[0:QC, :], ACT.Copy).then_inc(t_["qhi"], 1)
                    act.wait_ge(t_["kf2"], j + 1)
                    nc.scalar.activation(kh[:, 0, tok], kf[:, :], ACT.Copy).then_inc(t_["khi"], 1)

            @block.vector
            def _(dve):
                def over_batches(k):
                    return tabs[R:P, k, :].unsqueeze(1).to_broadcast([R, BT, T])

                for j in range(NT):
                    tok = slice(j * TILE, (j + 1) * TILE)
                    dve.wait_ge(t_["chi"], j + 1)
                    nc.vector.tensor_tensor(ctxT[:, 1], ctxf[:, :, :], ctxT[:, 0], ALU.subtract).then_inc(t_["clo"], 1)
                    dve.wait_ge(t_["xhi"], j + 1)
                    nc.vector.tensor_tensor(x1T[:, 1], xtP[:, :].rearrange("p (c t) -> p c t", c=CC), x1T[:, 0], ALU.subtract).then_inc(t_["xlo"], 1)
                    dve.wait_ge(t_["qhi"], j + 1)
                    nc.vector.tensor_tensor(qc[0:QC, 1, tok], qcP[0:QC, :], qc[0:QC, 0, tok], ALU.subtract).then_inc(t_["qlo"], 1)
                    dve.wait_ge(t_["kr"], j + 1)
                    nc.vector.tensor_tensor(kf[R:P, :].rearrange("p (b t) -> p b t", t=T), krP[R:P, :].rearrange("p (b t) -> p b t", t=T),
                                            over_batches(2), ALU.mult).then_inc(t_["krr"], 1)
                    nc.vector.tensor_tensor(ksw[R:P, :].rearrange("p (b t) -> p b t", t=T), ksP[R:P, :].rearrange("p (b t) -> p b t", t=T),
                                            over_batches(3), ALU.mult).then_inc(t_["kss"], 1)
                    dve.wait_ge(t_["kss"], j + 1)
                    nc.vector.tensor_tensor(kf[R:P, :], kf[R:P, :], ksw[R:P, :], ALU.add).then_inc(t_["kf2"], 1)
                    dve.wait_ge(t_["khi"], j + 1)
                    nc.vector.tensor_tensor(kh[:, 1, tok], kf[:, :], kh[:, 0, tok], ALU.subtract).then_inc(t_["klo"], 1)

    qh = sb("qh", [P, 2, BT, 2, T], F32)
    qhl = sb("qhl", [P, 2, BT * 2 * T], BF16)
    turn = sb("turn", [P, 2, BT, T], F32)
    scores = sb("x_scores", [P, BT, T], F32)
    probs = sb("x_probs", [P, BT, T], F32)
    probsT = sb("x_probsT", [P, TILE], F32)
    ntop, total, inv = sb("x_ntop", [P, BT], F32), sb("x_total", [P, BT], F32), sb("x_inv", [P, BT], F32)
    oT = sb("oT", [P, TILE], F32)
    oTl = sb("oTl", [P, TILE], BF16)

    def ps(name, n=TILE):
        return part.enter_context(nc.psum_tensor(name, [P, n], F32))

    qP = [ps("xq0"), ps("xq1"), ps("xq2")]
    sP, ptP, oP = ps("xsP"), ps("xptP"), ps("xoP")
    projP = ps("xprojP", PB * C)
    s_q, s_s, s_pt, s_o, s_proj = (sem("c_" + n) for n in ("q", "s", "pt", "o", "proj"))
    s_rot, s_qh, s_ql, s_bias, s_top, s_exp, s_inv, s_norm = (sem("c_" + n) for n in ("rot", "qh", "ql", "bias", "top", "exp", "inv", "norm"))
    s_pte, s_oa, s_ov, s_ol, s_acc = (sem("c_" + n) for n in ("pte", "oa", "ov", "ol", "acc"))

    def out_parts(src_rows):
        par = src_rows // KVC
        o4 = oP[:, :].rearrange("p (b i t) -> p b i t", b=PB, i=2)
        d4 = oT[:, :].rearrange("p (b q t) -> p b q t", b=PB, q=2)
        return [(d4[i * KVC:(i + 1) * KVC, :, par, :], o4[src_rows:src_rows + KVC, :, i, :]) for i in range(2)]

    with nc.Block() as block:
        @block.tensor
        def _(pe):
            def slot(g, j, n, has):
                if has(0):
                    wait(pe, s_rot, n)
                    for k in range(3):
                        for i, (u, z) in enumerate(PASSES):
                            last = nc.tensor.matmul(qP[k][:, :], at(WQ[:, u, :, k], g), qc[:, z, j * TILE:(j + 1) * TILE],
                                                    start=(i == 0), stop=(i == 2))
                        last.then_inc(s_q, 1)
                if has(1):
                    wait(pe, s_ql, n)
                    wait(pe, s_bias, n - 1)
                    jj, s = (j - 1) % NT, (j - 1) % 2
                    flat = qh[:, s].rearrange("p b i t -> p (b i t)")
                    for b in range(BT):
                        key = slice(jj * TILE + b * T, jj * TILE + (b + 1) * T)
                        for i, (u, z) in enumerate(PASSES):
                            q_part = flat[:, b * P:(b + 1) * P].bitcast(BF16)[:, 1::2] if u == 0 else qhl[:, s, b * P:(b + 1) * P]
                            last = nc.tensor.matmul(sP[:, b * T:(b + 1) * T], q_part, kh[:, z, key], start=(i == 0), stop=(i == 2))
                    last.then_inc(s_s, 1)
                if has(2):
                    wait(pe, s_norm, n - 1)
                    wait(pe, s_pte, n - 2)
                    for b in range(PB):
                        last = nc.tensor.transpose(ptP[:, b * P:(b + 1) * P], probs[:, 2 * b:2 * b + 2, :].rearrange("p b s -> p (b s)"), ident[:, :])
                    last.then_inc(s_pt, 1)
                if has(3):
                    wait(pe, s_ol, n - 2)
                    wait(pe, s_acc, n - 3)
                    wb = [at(WB[:, z], g if j >= 3 else g - 1) for z in range(2)]
                    for b in range(PB):
                        for i, (u, z) in enumerate(PASSES):
                            o_part = high(oT, slice(None), b * P, (b + 1) * P) if u == 0 else oTl[:, b * P:(b + 1) * P]
                            last = nc.tensor.matmul(projP[:, b * C:(b + 1) * C], o_part, wb[z], start=(i == 0), stop=(i == 2))
                    last.then_inc(s_proj, 1)
                if has(2):
                    wait(pe, s_pte, n - 1)
                    wait(pe, s_oa, n - 2)
                    wait(pe, s_ov, n - 2)
                    jj = (j - 2) % NT
                    for b in range(PB):
                        last = nc.tensor.matmul(oP[:, b * P:(b + 1) * P], KV[:, jj * PB + b, :], probsT[:, b * P:(b + 1) * P], start=True, stop=True)
                    last.then_inc(s_o, 1)

            slots(pe, slot, HP)

        @block.scalar
        def _(act):
            def slot(g, j, n, has):
                if has(2):
                    wait(act, s_pt, n - 1)
                    wait(act, s_o, n - 2)
                    nc.scalar.activation(probsT[:, :], ptP[:, :], ACT.Copy).then_inc(s_pte, 1)
                if has(1):
                    wait(act, s_top, n)
                    wait(act, s_inv, n - 1)
                    wait(act, s_pt, n - 1)
                    for b in range(BT):
                        last = nc.scalar.activation(probs[:, b, :], scores[:, b, :], ACT.Exp, bias=ntop[:, b:b + 1], accum_out=total[:, b:b + 1])
                    last.then_inc(s_exp, 1)
                if has(2):
                    wait(act, s_o, n - 1)
                    for dst, src in out_parts(0):
                        last = nc.scalar.activation(dst, src, ACT.Copy)
                    last.then_inc(s_oa, 1)

            nc.scalar.preload_act_table_set(EXP_LN)
            slots(act, slot, HP)

        @block.vector
        def _(dve):
            def slot(g, j, n, has):
                s = j % 2
                if has(2):
                    wait(dve, s_exp, n - 1)
                    nc.vector.reciprocal(inv[:, :], total[:, :]).then_inc(s_inv, 1)
                if has(0):
                    def cut(ap):
                        return ap.rearrange("p (b t) -> p b t", b=BT)

                    def tab(k, lo, hi):
                        return tabs[lo:hi, k, :].unsqueeze(1).to_broadcast([hi - lo, BT, T])

                    for i in range(2):
                        wait(dve, s_q, 3 * n + i + 1)
                        if i == 0:
                            wait(dve, s_s, n - 1)
                        nc.vector.tensor_tensor(qh[:, s, :, i, :], cut(qP[i][:, :]), tab(0, 0, P), ALU.mult)
                    wait(dve, s_q, 3 * n + 3)
                    wait(dve, s_qh, n)
                    nc.vector.tensor_tensor(turn[R:P, 0], cut(qP[2][R:P, :]), tab(1, R, P), ALU.mult)
                    nc.vector.tensor_tensor(turn[R:P, 1], cut(qP[2][0:R, :]), tab(1, 0, R), ALU.mult).then_inc(s_rot, 1)
                    wait(dve, s_rot, n + 1)
                    rope = qh[R:P, s].rearrange("p b i t -> p i b t")
                    nc.vector.tensor_tensor(rope, rope, turn[R:P, :, :, :], ALU.add).then_inc(s_qh, 1)
                if has(1):
                    jj = (j - 1) % NT
                    wait(dve, s_s, n)
                    nc.vector.tensor_tensor(scores[:, :, :], sP[:, :].rearrange("p (b s) -> p b s", b=BT), mask[:, jj * BT:(jj + 1) * BT, :], ALU.add).then_inc(s_bias, 1)
                    wait(dve, s_bias, n)
                    nc.vector.tensor_reduce(ntop[:, :], scores[:, :, :], AX, ALU.max, negate=True).then_inc(s_top, 1)
                if has(3):
                    acc = X[:, ((j - 3) % NT) * PB:((j - 3) % NT + 1) * PB, :]
                    wait(dve, s_proj, n - 2)
                    wait(dve, s_acc, n - 3)
                    nc.vector.tensor_tensor(acc, projP[:, :].rearrange("p (b c) -> p b c", b=PB), acc, ALU.add).then_inc(s_acc, 1)
                if has(2):
                    wait(dve, s_o, n - 1)
                    for dst, src in out_parts(KVC):
                        last = nc.vector.tensor_copy(dst, src)
                    last.then_inc(s_ov, 1)

            slots(dve, slot, HP)

        @block.gpsimd
        def _(pool):
            def slot(g, j, n, has):
                if has(2):
                    wait(pool, s_inv, n - 1)
                    nc.gpsimd.tensor_tensor(probs[:, :, :], probs[:, :, :], inv[:, :].unsqueeze(2).to_broadcast([P, BT, T]), ALU.mult).then_inc(s_norm, 1)
                if has(3):
                    wait(pool, s_oa, n - 2)
                    wait(pool, s_ov, n - 2)
                    wait(pool, s_proj, n - 3)
                    nc.gpsimd.tensor_tensor(oTl[:, :], oT[:, :], high(oT, slice(None), 0, TILE), ALU.subtract).then_inc(s_ol, 1)
                if has(0):
                    s = j % 2
                    wait(pool, s_qh, n + 1)
                    wait(pool, s_s, n - 1)
                    flat = qh[:, s].rearrange("p b i t -> p (b i t)")
                    nc.gpsimd.tensor_tensor(qhl[:, s, :], flat, flat.bitcast(BF16)[:, 1::2], ALU.subtract).then_inc(s_ql, 1)

            slots(pool, slot, HP)


def feed_forward(nc, a, X, ident, sem, sb, part):
    wg, wu, wd = sb("wg", [P, CC, DFF], BF16), sb("wu", [P, CC, DFF], BF16), sb("wd", [P, FC, C], BF16)
    xqT = sb("xqT", [P, CC, TOK], BF16)
    wsc = sb("wsc", [P, 3], F32)
    xsc = sb("xsc", [P, NB], F32)
    gsc, usc = sb("gsc", [P, NB], F32), sb("usc", [P, NB], F32)
    identb = sb("identb", [P, P], BF16)
    magic = sb("magic", [P, 1], F32)

    with ExitStack() as own:
        def tmp(name, shape, dt=F32):
            return own.enter_context(nc.sbuf_tensor(name, shape, dt))

        wf = [tmp("wgf", [P, CC, DFF]), tmp("wuf", [P, CC, DFF]), tmp("wdf", [P, FC, C])]
        wq = [wg, wu, wd]
        ones = tmp("onesf", [P, P])
        sums = tmp("wsums", [P, 3])
        winv, xinv = tmp("winv", [P, 3]), tmp("xinv", [P, NB])
        xs, xq = tmp("xs", [P, NB, C]), tmp("xq", [P, NB, C], BF16)
        sumP = own.enter_context(nc.psum_tensor("wsumP", [P, TILE], F32))
        tP = [own.enter_context(nc.psum_tensor(f"xqP{i}", [P, CC * TILE], BF16)) for i in range(2)]
        s_ld, s_d, s_ones, s_sum, s_sumP, s_t, s_te, s_xq, s_id = (sem("fp_" + n) for n in ("ld", "dve", "ones", "sum", "sumP", "t", "te", "xq", "id"))
        with nc.Block() as block:
            @block.sync
            def _(sp):
                sp.dma_start(wf[0][:, :, :], a["wgT"].rearrange("(c p) n -> p c n", p=P)).then_inc(s_ld, 16)
                sp.dma_start(wf[1][:, :, :], a["wuT"].rearrange("(c p) n -> p c n", p=P)).then_inc(s_ld, 16)
                sp.dma_start(wf[2][:, :, :], a["wdT"].rearrange("(c p) n -> p c n", p=P)).then_inc(s_ld, 16)

            @block.vector
            def _(dve):
                done = [0]

                def then(ins):
                    done[0] += 1
                    ins.then_inc(s_d, 1)
                    dve.wait_ge(s_d, done[0])

                nc.vector.memset(ones[:, :], 1.0).then_inc(s_ones, 1)
                nc.vector.memset(magic[:, :], MAGIC)
                nc.vector.tensor_copy(identb[:, :], ident[:, :]).then_inc(s_id, 1)
                then(nc.vector.tensor_reduce(xsc[:, :], X[:, :, :], AX, ALU.max, apply_absolute_value=True))
                then(nc.vector.tensor_scalar(xsc[:, :], xsc[:, :], EPS, 1.0 / 127.0, ALU.max, ALU.mult))
                then(nc.vector.reciprocal(xinv[:, :], xsc[:, :]))
                then(nc.vector.tensor_tensor(xs[:, :, :], X[:, :, :], xinv[:, :].unsqueeze(2).to_broadcast([P, NB, C]), ALU.mult))
                then(nc.vector.tensor_scalar(xs[:, :, :], xs[:, :, :], MAGIC, None, ALU.add))
                nc.vector.tensor_scalar(xq[:, :, :], xs[:, :, :], MAGIC, None, ALU.subtract).then_inc(s_xq, 1)
                dve.wait_ge(s_ld, 3 * 16)
                for k in range(3):
                    nc.vector.tensor_reduce(sums[:, k:k + 1], wf[k][:, :, :].rearrange("p a b -> p (a b)"), AX, ALU.add,
                                            apply_absolute_value=True).then_inc(s_sum, 1)
                dve.wait_ge(s_sumP, 1)
                then(nc.vector.tensor_scalar(wsc[:, :], sumP[:, 0:3], 1.0 / (C * DFF), EPS, ALU.mult, ALU.add))
                then(nc.vector.reciprocal(winv[:, :], wsc[:, :]))
                for k in range(3):
                    then(nc.vector.tensor_scalar(wf[k][:, :, :], wf[k][:, :, :], winv[:, k:k + 1], MAGIC, ALU.mult, ALU.add))
                    then(nc.vector.tensor_scalar(wf[k][:, :, :], wf[k][:, :, :], MAGIC, 1.0, ALU.subtract, ALU.min))
                    nc.vector.tensor_scalar(wq[k][:, :, :], wf[k][:, :, :], -1.0, None, ALU.max)
                nc.vector.tensor_scalar(gsc[:, :], xsc[:, :], wsc[:, 0:1], None, ALU.mult)
                nc.vector.tensor_scalar(usc[:, :], xsc[:, :], wsc[:, 1:2], None, ALU.mult)

            @block.tensor
            def _(pe):
                pe.wait_ge(s_xq, 1)
                pe.wait_ge(s_id, 1)
                for j in range(NT):
                    if j >= 2:
                        pe.wait_ge(s_te, j - 1)
                    for c in range(CC):
                        for b in range(PB):
                            last = nc.tensor.transpose(tP[j % 2][:, c * TILE + b * P:c * TILE + (b + 1) * P],
                                                       xq[:, j * PB + b, c * P:(c + 1) * P], identb[:, :])
                    last.then_inc(s_t, 1)
                pe.wait_ge(s_sum, 3)
                pe.wait_ge(s_ones, 1)
                nc.tensor.matmul(sumP[:, 0:3], ones[:, :], sums[:, :], start=True, stop=True).then_inc(s_sumP, 1)

            @block.scalar
            def _(act):
                for j in range(NT):
                    act.wait_ge(s_t, j + 1)
                    nc.scalar.activation(xqT[:, :, j * TILE:(j + 1) * TILE], tP[j % 2][:, :].rearrange("p (c t) -> p c t", c=CC), ACT.Copy).then_inc(s_te, 1)

    UN = 4
    sig, hs, hm = sb("sig", [P, DFF], F32), sb("hs", [P, DFF], F32), sb("hm", [P, DFF], F32)
    hq = sb("hq", [P, 2, DFF], BF16)
    hqT = sb("hqT", [P, DFF], BF16)
    hsc, hinv = sb("hsc", [P, UN], F32), sb("hinv", [P, UN], F32)
    dsc = sb("dsc", [P, UN], F32)
    gP, uP = (part.enter_context(nc.psum_tensor(n, [P, DFF], F32)) for n in ("gP", "uP"))
    tP = part.enter_context(nc.psum_tensor("hqP", [P, DFF], BF16))
    dP = part.enter_context(nc.psum_tensor("dP", [P, TILE], F32))
    s_g, s_u, s_t, s_dn = (sem("f_" + n) for n in ("g", "u", "t", "dn"))
    s_sig, s_h, s_max, s_sc, s_inv, s_dsc, s_hm, s_hq, s_te, s_y = (sem("f_" + n) for n in ("sig", "h", "max", "sc", "inv", "dsc", "hm", "hq", "te", "y"))

    with nc.Block() as block:
        @block.tensor
        def _(pe):
            def slot(g, j, n, has):
                if has(0):
                    for w, dst, free, ready in ((wg, gP, s_sig, s_g), (wu, uP, s_h, s_u)):
                        wait(pe, free, n)
                        for f in range(DFF // TILE):
                            for c in range(CC):
                                x = xqT[:, c, n * P:(n + 1) * P] if isinstance(n, int) else xqT[:, c, bass.ds(n * P, P)]
                                last = nc.tensor.matmul(dst[:, f * TILE:(f + 1) * TILE], x, w[:, c, f * TILE:(f + 1) * TILE],
                                                        start=(c == 0), stop=(c == CC - 1))
                        last.then_inc(ready, 1)
                if has(2):
                    wait(pe, s_hq, n - 1)
                    wait(pe, s_te, n - 2)
                    for f in range(FC):
                        last = nc.tensor.transpose(tP[:, f * P:(f + 1) * P], hq[:, j % 2, f * P:(f + 1) * P], identb[:, :])
                    last.then_inc(s_t, 1)
                    wait(pe, s_te, n - 1)
                    wait(pe, s_y, n - 2)
                    for f in range(FC):
                        last = nc.tensor.matmul(dP[:, 0:C], hqT[:, f * P:(f + 1) * P], wd[:, f, :], start=(f == 0), stop=(f == FC - 1))
                    last.then_inc(s_dn, 1)

            slots(pe, slot, NB // UN, UN, 3)

        @block.scalar
        def _(act):
            def slot(g, j, n, has):
                if has(0):
                    wait(act, s_g, n + 1)
                    wait(act, s_h, n)
                    nc.scalar.activation(sig[:, :], gP[:, :], ACT.Sigmoid, scale=gsc[:, n:n + 1] if isinstance(n, int) else gsc[:, bass.ds(n, 1)]).then_inc(s_sig, 1)
                if has(1):
                    jj = (j - 1) % UN
                    wait(act, s_inv, n)
                    wait(act, s_hq, n - 1)
                    nc.scalar.activation(hm[:, :], hs[:, :], ACT.Identity, bias=magic[:, :], scale=hinv[:, jj:jj + 1]).then_inc(s_hm, 1)
                    wait(act, s_hm, n)
                    wait(act, s_t, n - 2)
                    nc.scalar.activation(hq[:, (j - 1) % 2, :], hm[:, :], ACT.Copy, bias=-MAGIC).then_inc(s_hq, 1)

            slots(act, slot, NB // UN, UN, 3)

        @block.vector
        def _(dve):
            def slot(g, j, n, has):
                if has(0):
                    wait(dve, s_sig, n + 1)
                    wait(dve, s_u, n + 1)
                    wait(dve, s_hm, n)
                    nc.vector.scalar_tensor_tensor(hs[:, :], uP[:, :], usc[:, n:n + 1] if isinstance(n, int) else usc[:, bass.ds(n, 1)], sig[:, :],
                                                   ALU.mult, ALU.mult).then_inc(s_h, 1)
                    wait(dve, s_h, n + 1)
                    nc.vector.tensor_reduce(hsc[:, j:j + 1], hs[:, :], AX, ALU.max, apply_absolute_value=True).then_inc(s_max, 1)
                    wait(dve, s_max, n + 1)
                    nc.vector.tensor_scalar(hsc[:, j:j + 1], hsc[:, j:j + 1], EPS, 1.0 / 127.0, ALU.max, ALU.mult).then_inc(s_sc, 1)
                    wait(dve, s_sc, n + 1)
                    nc.vector.reciprocal(hinv[:, j:j + 1], hsc[:, j:j + 1]).then_inc(s_inv, 1)
                    nc.vector.tensor_scalar(dsc[:, j:j + 1], hsc[:, j:j + 1], wsc[:, 2:3], None, ALU.mult).then_inc(s_dsc, 1)
                if has(2):
                    jj = (j - 2) % UN
                    wait(dve, s_t, n - 1)
                    wait(dve, s_dn, n - 2)
                    nc.vector.tensor_copy(hqT[:, :], tP[:, :]).then_inc(s_te, 1)
                    wait(dve, s_dn, n - 1)
                    wait(dve, s_dsc, n - 1)
                    x = at(X, n - 2)
                    nc.vector.scalar_tensor_tensor(x, dP[:, 0:C], dsc[:, jj:jj + 1], x, ALU.mult, ALU.add).then_inc(s_y, 1)

            slots(dve, slot, NB // UN, UN, 3)


def constants():
    import numpy as np

    t = np.arange(P)
    same = (t[:, None] // T) == (t[None, :] // T)
    dist = (t[:, None] % T) - (t[None, :] % T)
    slopes = np.array([2.0 ** (-8.0 * (h + 1) / H) for h in range(H)])
    bias = np.where(dist >= 0, -dist[:, None, :].transpose(1, 0, 2) * slopes[:, None, None], NEG)
    bias = np.where(same, bias, NEG).transpose(1, 0, 2).reshape(P, H * P)
    half = R // 2
    freq = 1.0 / 10000.0 ** (np.arange(half) / half)
    ang = (np.arange(T)[:, None] * freq).T
    cos, sin = np.concatenate([np.cos(ang)] * 2), np.concatenate([-np.sin(ang), np.sin(ang)])
    one, scale = np.ones((KVC, T)), 1.0 / np.sqrt(D + R)
    rope = np.concatenate([np.concatenate([one, cos]) * scale, np.concatenate([sin, sin]) * scale,
                           np.concatenate([cos, cos]), np.concatenate([sin, sin])], axis=1)
    keys = np.tile(np.arange(T) + LOOKBACK / 2, (P, 1))
    return {"ident": np.eye(P, dtype=np.float32), "bias": bias.astype(np.float32),
            "rope": rope.astype(np.float32), "keys": keys.astype(np.float32)}


def kernel(**inputs):
    import numpy as np
    import concourse.bacc as bacc
    from concourse.bass_utils import run_bass_kernel_spmd

    nc = bacc.Bacc("TRN2", target_bir_lowering=False, num_devices=1)
    x = np.asarray(inputs["x"])
    arrays = {"x": x.reshape(TOK, C), "xT": x.reshape(TOK, C).T,
              "ctxT": np.asarray(inputs["ctx_2048"]).reshape(TOK, C).T,
              "segT": np.asarray(inputs["itok_BxS_0_1023"]).T}
    for name in ("L0_attn_Wq", "L0_attn_Wk", "L0_attn_Wv", "L0_attn_Wproj", "L0_attn_q_rms_w", "L0_attn_k_rms_w",
                 "L0_attn_subln_w", "L0_xattn_W_dq", "L0_xattn_W_kvc", "L0_xattn_W_o", "L0_xattn_W_qr"):
        arrays[name] = np.asarray(inputs[name])
    swap = np.concatenate([np.arange(R // 2, R), np.arange(R // 2)])
    W_qr, W_kr = np.asarray(inputs["L0_xattn_W_qr"]), np.asarray(inputs["L0_xattn_W_kr"])
    arrays["qrs"] = W_qr.reshape(QC, H, R)[:, :, swap].reshape(QC, H * R)
    arrays["wkr"] = np.concatenate([W_kr, W_kr[:, swap]], axis=1)
    for short, name in (("uqT", "L0_xattn_W_uq"), ("ukT", "L0_xattn_W_uk"), ("uvT", "L0_xattn_W_uv"),
                        ("wgT", "L0_ffn_w_gate"), ("wuT", "L0_ffn_w_up"), ("wdT", "L0_ffn_w_down")):
        arrays[short] = np.asarray(inputs[name]).T
    arrays.update(constants())
    arrays = {n: np.ascontiguousarray(v) for n, v in arrays.items()}
    a = {n: nc.dram_tensor("in_" + n, v.shape, mybir.dt.from_np(v.dtype), kind="ExternalInput").ap() for n, v in arrays.items()}
    out = nc.dram_tensor("out", (TOK, C), F32, kind="ExternalOutput").ap()
    build(nc, a, out)
    r = run_bass_kernel_spmd(nc, [{"in_" + n: v for n, v in arrays.items()}], core_ids=[0])
    return r.results[0]["out"].reshape(B, T, C)
```

```python
import concourse.bass as bass
from concourse import mybir
from concourse.alu_op_type import AluOpType as ALU
from contextlib import ExitStack

F32 = mybir.dt.float32
BF16 = mybir.dt.bfloat16
I32 = mybir.dt.int32
ACT = mybir.ActivationFunctionType
AX = mybir.AxisListType.X

P = 128
B, T, C = 64, 64, 256
TOK = B * T
H, D = 16, 128
CC = C // P
TILE = 512
NT = TOK // TILE
PB = TILE // P
NB = TOK // P
BT = TILE // T
KVC, QC, R = 64, 96, 64
HP = H // 2
DFF = 1024
FC = DFF // P
EPS = 1e-5
NEG = -1e30
EXP_LN = "natural_log_exp_and_others"
LOOKBACK = 8
MAGIC = 12582912.0

PASSES = ((0, 0), (0, 1), (1, 0))


def wait(eng, sem, count):
    if not isinstance(count, int) or count > 0:
        eng.wait_ge(sem, count)


def high(tile, rows, lo, hi):
    return tile[rows, lo:hi].bitcast(BF16)[:, 1::2]


def slots(eng, slot, heads, inner=NT, lags=4):
    last = heads * inner
    for j in range(inner):
        slot(0, j, j, lambda lag: lag <= j)
    with eng.Fori(1, heads) as h:
        for j in range(inner):
            slot(h, j, h * inner + j, lambda lag: True)
    for j in range(lags - 1):
        slot(heads, j, last + j, lambda lag: lag > j)


def at(tile, i):
    return tile[:, i] if isinstance(i, int) else tile[:, bass.ds(i, 1)].squeeze(1)


def build(nc, a, out):
    ctx = ExitStack()
    with ctx:
        def sem(name):
            return ctx.enter_context(nc.semaphore(name))

        def sb(name, shape, dt, where=ctx):
            return where.enter_context(nc.sbuf_tensor(name, shape, dt))

        X = sb("X", [P, NB, C], F32)
        ident = sb("ident", [P, P], F32)
        eps_col = sb("eps_col", [P, 1], F32)
        with ExitStack() as part:
            self_attention(nc, a, X, ident, eps_col, sem, lambda n, s, d: sb(n, s, d, part), part)
        with ExitStack() as part:
            layer_norm(nc, X, eps_col, sem, lambda n, s, d: sb(n, s, d, part), "ln1")
        with ExitStack() as part:
            cross_attention(nc, a, X, ident, sem, lambda n, s, d: sb(n, s, d, part), part)
        with ExitStack() as part:
            layer_norm(nc, X, eps_col, sem, lambda n, s, d: sb(n, s, d, part), "ln2")
        with ExitStack() as part:
            feed_forward(nc, a, X, ident, sem, lambda n, s, d: sb(n, s, d, part), part)
        with ExitStack() as part:
            layer_norm(nc, X, eps_col, sem, lambda n, s, d: sb(n, s, d, part), "ln3", out)


def self_attention(nc, a, X, ident, eps_col, sem, sb, part):
    W = sb("W", [P, 2, 3, CC, H * D], BF16)
    xT = sb("xT", [P, 2, CC, TOK], BF16)
    Wp = sb("Wp", [P, 2, H, C], BF16)
    bias = sb("bias", [P, H, P], F32)
    qkw = sb("qkw", [P, 4], F32)
    ones = sb("ones", [P, P], BF16)
    eps_qy = sb("eps_qy", [P, 2, 2 * PB], F32)

    with ExitStack() as own:
        stage = own.enter_context(nc.sbuf_tensor("stage", [P, 2, 2 * CC * TOK // 4], F32))
        s_const, s_x = sem("s_const"), sem("s_x")
        s_st = [sem("s_stage0"), sem("s_stage1")]
        s_hi, s_lo, s_scaled, s_w = sem("s_stage_hi"), sem("s_stage_lo"), sem("s_wproj_scaled"), sem("s_qkw")
        half = TOK // 2
        ROW = CC * H * D
        loads = []
        for i in range(2):
            loads.append((a["xT"].rearrange("(c p) t -> p c t", p=P)[:, :, i * half:(i + 1) * half],
                          [xT[:, k, :, i * half:(i + 1) * half] for k in range(2)], CC))
        for i, n in enumerate(("L0_attn_Wq", "L0_attn_Wk", "L0_attn_Wv")):
            loads.append((a[n].rearrange("(c p) n -> p c n", p=P), [W[:, k, i] for k in range(2)], CC))
        loads.append((a["L0_attn_Wproj"].rearrange("(h p) n -> p h n", p=P), [Wp[:, k] for k in range(2)], H))

        def staged(i):
            return stage[:, i % 2].rearrange("p (c n) -> p c n", c=loads[i][2])

        with nc.Block() as block:
            @block.sync
            def _(sp):
                for i, (src, _, _) in enumerate(loads):
                    if i >= 2:
                        sp.wait_ge(s_lo, i - 1)
                    sp.dma_start(staged(i), src).then_inc(s_st[i % 2], 16)
                    if i == 0:
                        for k, n in enumerate(("q_rms_w", "k_rms_w", "subln_w")):
                            sp.dma_start(qkw[:, k:k + 1], a["L0_attn_" + n].rearrange("(p o) -> p o", o=1)).then_inc(s_const, 16)
                        sp.dma_start(ident[:, :], a["ident"]).then_inc(s_const, 16)
                        sp.dma_start(bias[:, :, :], a["bias"].rearrange("p (h n) -> p h n", h=H)).then_inc(s_const, 16)
                sp.dma_start(X[:, :, :], a["x"].rearrange("(n p) c -> p n c", p=P)).then_inc(s_x, 16)
                sp.wait_ge(s_x, 16)

            @block.scalar
            def _(act):
                for i, (_, dst, _) in enumerate(loads):
                    act.wait_ge(s_st[i % 2], 16 * (i // 2 + 1))
                    if i == len(loads) - 1:
                        act.wait_ge(s_scaled, 1)
                    nc.scalar.activation(dst[0], staged(i), ACT.Copy).then_inc(s_hi, 1)

            @block.vector
            def _(dve):
                nc.vector.memset(ones[:, :], 1.0)
                nc.vector.memset(eps_col[:, :], EPS)
                nc.vector.memset(eps_qy[:, :, :], EPS)
                dve.wait_ge(s_const, 5 * 16)
                nc.vector.scalar_tensor_tensor(qkw[:, 3:4], qkw[:, 0:1], D ** -0.5, qkw[:, 1:2],
                                               ALU.mult, ALU.mult).then_inc(s_w, 1)
                for i, (_, dst, _) in enumerate(loads):
                    dve.wait_ge(s_st[i % 2], 16 * (i // 2 + 1))
                    if i == len(loads) - 1:
                        nc.vector.tensor_scalar(stage[:, i % 2], stage[:, i % 2], qkw[:, 2:3], None,
                                                ALU.mult).then_inc(s_scaled, 1)
                    dve.wait_ge(s_hi, i + 1)
                    nc.vector.tensor_tensor(dst[1], staged(i), dst[0], ALU.subtract).then_inc(s_lo, 1)

    q_sq, k_sq, y_sq = sb("q_sq", [P, TILE], F32), sb("k_sq", [P, TILE], F32), sb("y_sq", [P, TILE], F32)
    q_sql, k_sql, y_sql = sb("q_sql", [P, TILE], BF16), sb("k_sql", [P, TILE], BF16), sb("y_sql", [P, TILE], BF16)
    q, rk, kn = sb("q", [P, 2, TILE], F32), sb("rk", [P, TILE], F32), sb("kn", [P, TILE], F32)
    y, yl = sb("y", [P, TILE], F32), sb("yl", [P, TILE], BF16)
    VB = 4
    v = sb("v", [P, VB, PB, D], F32)
    scores = sb("scores", [P, PB, P], F32)
    probs = sb("probs", [P, PB, P], F32)
    probsT = sb("probsT", [P, TILE], F32)
    ntop, total = sb("ntop", [P, PB], F32), sb("total", [P, PB], F32)
    mean_sq, r = sb("mean_sq", [P, 2 * PB], F32), sb("r", [P, 2 * PB], F32)

    def ps(name, n=TILE):
        return part.enter_context(nc.psum_tensor(name, [P, n], F32))

    qP, kP, kssP, svP, pyP, qyssP = ps("qP"), ps("kP"), ps("kssP"), ps("svP"), ps("pyP"), ps("qyssP")
    projP = ps("projP", PB * C)

    s_q, s_k, s_v, s_s, s_pt, s_y, s_proj = (sem("a_" + n) for n in ("q", "k", "v", "s", "pt", "y", "proj"))
    s_qss, s_kss, s_yss = sem("a_qss"), sem("a_kss"), sem("a_yss")
    s_qsq, s_ksq, s_ysq = sem("a_qsq"), sem("a_ksq"), sem("a_ysq")
    s_qsql, s_ksql, s_ysql = sem("a_qsql"), sem("a_ksql"), sem("a_ysql")
    s_kln, s_rk, s_kn, s_mean, s_rln, s_r = (sem("a_" + n) for n in ("kln", "rk", "kn", "mean", "rln", "r"))
    s_qe, s_ve, s_ye, s_yl, s_pte = (sem("a_" + n) for n in ("qe", "ve", "ye", "yl", "pte"))
    s_bias, s_top, s_exp, s_eps, s_acc = (sem("a_" + n) for n in ("bias", "top", "exp", "eps", "acc"))

    with nc.Block() as block:
        @block.tensor
        def _(pe):
            def project(dst, w, h, tok):
                last = None
                for c in range(CC):
                    for i, (u, z) in enumerate(PASSES):
                        last = nc.tensor.matmul(dst[:, :], W[:, u, w, c, bass.ds(h * D, D)], xT[:, z, c, tok],
                                                start=(c == 0 and i == 0), stop=(c == CC - 1 and i == 2))
                return last

            def row_square_sums(col, sq, low):
                last = None
                for b in range(PB):
                    for i, part_ in enumerate((high(sq, slice(None), b * P, (b + 1) * P), low[:, b * P:(b + 1) * P])):
                        last = nc.tensor.matmul(qyssP[:, col + b:col + b + 1], part_, ones[:, 0:1], start=(i == 0), stop=(i == 1))
                return last

            def slot(h, j, n, has):
                tok = slice(j * TILE, (j + 1) * TILE)
                if has(0):
                    wait(pe, s_qe, n)
                    project(qP, 0, h, tok).then_inc(s_q, 1)
                    wait(pe, s_kn, n)
                    project(kP, 1, h, tok).then_inc(s_k, 1)
                if has(3):
                    wait(pe, s_ysql, n - 2)
                    wait(pe, s_mean, n - 1)
                    row_square_sums(PB, y_sq, y_sql).then_inc(s_yss, 1)
                if has(1):
                    wait(pe, s_qe, n)
                    wait(pe, s_kn, n)
                    wait(pe, s_ve, n)
                    for b in range(PB):
                        blk = slice(b * P, (b + 1) * P)
                        last = nc.tensor.matmul(svP[:, blk], q[:, (j - 1) % 2, blk], kn[:, blk], start=True, stop=True)
                    last.then_inc(s_s, 1)
                if has(2):
                    wait(pe, s_exp, n - 1)
                    wait(pe, s_ye, n - 2)
                    for b in range(PB):
                        last = nc.tensor.transpose(pyP[:, b * P:(b + 1) * P], probs[:, b, :], ident[:, :])
                    last.then_inc(s_pt, 1)
                if has(3):
                    wait(pe, s_yl, n - 2)
                    wait(pe, s_acc, n - 3)
                    wp = [at(Wp[:, z], h if j >= 3 else h - 1) for z in range(2)]
                    for b in range(PB):
                        for i, (u, z) in enumerate(PASSES):
                            y_part = high(y, slice(None), b * P, (b + 1) * P) if u == 0 else yl[:, b * P:(b + 1) * P]
                            last = nc.tensor.matmul(projP[:, b * C:(b + 1) * C], y_part, wp[z],
                                                    start=(i == 0), stop=(i == 2))
                    last.then_inc(s_proj, 1)
                if has(0):
                    wait(pe, s_qsql, n + 1)
                    wait(pe, s_mean, n)
                    row_square_sums(0, q_sq, q_sql).then_inc(s_qss, 1)
                    wait(pe, s_ksql, n + 1)
                    nc.tensor.matmul(kssP[:, :], ones[:, :], high(k_sq, slice(None), 0, TILE), start=True, stop=False)
                    nc.tensor.matmul(kssP[:, :], ones[:, :], k_sql[:, :], start=False, stop=True).then_inc(s_kss, 1)
                if has(2):
                    wait(pe, s_pte, n - 1)
                    vb = (j - 2) % VB
                    for b in range(PB):
                        last = nc.tensor.matmul(pyP[:, b * P:(b + 1) * P], v[:, vb, b, :], probsT[:, b * P:(b + 1) * P],
                                                start=True, stop=True)
                    last.then_inc(s_y, 1)
                if has(0):
                    wait(pe, s_bias, n)
                    for b in range(PB):
                        for c in range(CC):
                            for i, (u, z) in enumerate(PASSES):
                                last = nc.tensor.matmul(svP[:, b * D:(b + 1) * D],
                                                        xT[:, u, c, j * TILE + b * P:j * TILE + (b + 1) * P],
                                                        W[:, z, 2, c, bass.ds(h * D, D)],
                                                        start=(c == 0 and i == 0), stop=(c == CC - 1 and i == 2))
                    last.then_inc(s_v, 1)

            slots(pe, slot, H)

        @block.scalar
        def _(act):
            def slot(h, j, n, has):
                if has(0):
                    wait(act, s_q, n + 1)
                    wait(act, s_qss, n)
                    nc.scalar.activation(q_sq[:, :], qP[:, :], ACT.Square).then_inc(s_qsq, 1)
                    wait(act, s_s, n - 1)
                    nc.scalar.activation(q[:, j % 2, :], qP[:, :], ACT.Copy).then_inc(s_qe, 1)
                    wait(act, s_k, n + 1)
                    wait(act, s_kss, n)
                    nc.scalar.activation(k_sq[:, :], kP[:, :], ACT.Square).then_inc(s_ksq, 1)
                if has(1) or has(3):
                    cols = slice(0 if has(1) else PB, 2 * PB if has(3) else PB)
                    wait(act, s_mean, n)
                    if has(2):
                        wait(act, s_bias, n - 1)
                    wait(act, s_acc, n - 3)
                    nc.scalar.activation(r[:, cols], mean_sq[:, cols], ACT.Ln).then_inc(s_rln, 1)
                    wait(act, s_rln, n)
                    nc.scalar.activation(r[:, cols], r[:, cols], ACT.Exp, scale=-0.5).then_inc(s_r, 1)
                if has(2):
                    wait(act, s_pt, n - 1)
                    wait(act, s_y, n - 2)
                    nc.scalar.activation(probsT[:, :], pyP[:, :], ACT.Copy).then_inc(s_pte, 1)
                if has(1):
                    wait(act, s_top, n)
                    wait(act, s_pt, n - 1)
                    wait(act, s_eps, n - 1)
                    for b in range(PB):
                        last = nc.scalar.activation(probs[:, b, :], scores[:, b, :], ACT.Exp, bias=ntop[:, b:b + 1], accum_out=total[:, b:b + 1])
                    last.then_inc(s_exp, 1)
                if has(0):
                    wait(act, s_kss, n + 1)
                    wait(act, s_kn, n)
                    nc.scalar.activation(rk[:, :], kssP[:, :], ACT.Ln, bias=eps_col[:, :], scale=1.0 / D).then_inc(s_kln, 1)
                    wait(act, s_kln, n + 1)
                    nc.scalar.activation(rk[:, :], rk[:, :], ACT.Exp, scale=-0.5).then_inc(s_rk, 1)
                if has(2):
                    wait(act, s_y, n - 1)
                    wait(act, s_yss, n - 2)
                    nc.scalar.activation(y_sq[:, :], pyP[:, :], ACT.Square).then_inc(s_ysq, 1)
                    wait(act, s_proj, n - 2)
                    nc.scalar.activation(y[:, :], pyP[:, :], ACT.Copy).then_inc(s_ye, 1)

            nc.scalar.preload_act_table_set(EXP_LN)
            slots(act, slot, H)

        @block.vector
        def _(dve):
            def slot(h, j, n, has):
                if has(1):
                    wait(dve, s_v, n)
                    nc.vector.tensor_copy(v[:, (j - 1) % VB], svP[:, :].rearrange("p (b d) -> p b d", b=PB)).then_inc(s_ve, 1)
                if has(1) or has(3):
                    cols = slice(0 if has(1) else PB, 2 * PB if has(3) else PB)
                    if has(1):
                        wait(dve, s_qss, n)
                    if has(3):
                        wait(dve, s_yss, n - 2)
                        wait(dve, s_eps, n - 2)
                    wait(dve, s_rln, n - 1)
                    nc.vector.scalar_tensor_tensor(mean_sq[:, cols], qyssP[:, cols], 1.0 / D, eps_qy[:, (j - 1) % 2, cols],
                                                   ALU.mult, ALU.add).then_inc(s_mean, 1)
                if has(1):
                    row = at(bias, h if j >= 1 else h - 1)
                    wait(dve, s_s, n)
                    wait(dve, s_r, n)
                    wait(dve, s_exp, n - 1)
                    for b in range(PB):
                        last = nc.vector.scalar_tensor_tensor(scores[:, b, :], svP[:, b * P:(b + 1) * P], r[:, b:b + 1], row, ALU.mult, ALU.add)
                    last.then_inc(s_bias, 1)
                    wait(dve, s_bias, n)
                    nc.vector.tensor_reduce(ntop[:, :], scores[:, :, :], AX, ALU.max, negate=True).then_inc(s_top, 1)
                if has(3):
                    jj = (j - 3) % NT
                    wait(dve, s_proj, n - 2)
                    wait(dve, s_r, n)
                    wait(dve, s_acc, n - 3)
                    for b in range(PB):
                        acc = X[:, jj * PB + b, :]
                        last = nc.vector.scalar_tensor_tensor(acc, projP[:, b * C:(b + 1) * C], r[:, PB + b:PB + b + 1], acc, ALU.mult, ALU.add)
                    last.then_inc(s_acc, 1)
                if has(1):
                    wait(dve, s_exp, n)
                    wait(dve, s_mean, n)
                    nc.vector.scalar_tensor_tensor(eps_qy[:, (j - 1) % 2, PB:2 * PB], total[:, :], EPS, total[:, :], ALU.mult, ALU.mult).then_inc(s_eps, 1)
                if has(0):
                    wait(dve, s_rk, n + 1)
                    wait(dve, s_s, n)
                    nc.vector.scalar_tensor_tensor(kn[:, :], kP[:, :], qkw[:, 3:4], rk[:, :], ALU.mult, ALU.mult).then_inc(s_kn, 1)

            slots(dve, slot, H)

        @block.gpsimd
        def _(pool):
            def low_part(dst, src):
                return nc.gpsimd.tensor_tensor(dst[:, :], src[:, :], high(src, slice(None), 0, TILE), ALU.subtract)

            def slot(h, j, n, has):
                if has(3):
                    wait(pool, s_ysq, n - 2)
                    wait(pool, s_yss, n - 3)
                    low_part(y_sql, y_sq).then_inc(s_ysql, 1)
                    wait(pool, s_ye, n - 2)
                    wait(pool, s_proj, n - 3)
                    low_part(yl, y).then_inc(s_yl, 1)
                if has(0):
                    wait(pool, s_qsq, n + 1)
                    wait(pool, s_qss, n)
                    low_part(q_sql, q_sq).then_inc(s_qsql, 1)
                    wait(pool, s_ksq, n + 1)
                    wait(pool, s_kss, n)
                    low_part(k_sql, k_sq).then_inc(s_ksql, 1)

            slots(pool, slot, H)


def layer_norm(nc, X, eps_col, sem, sb, tag, out=None):
    stats = sb(tag + "_stats", [P, NB, 6], F32)
    mean, var = sb(tag + "_mean", [P, NB], F32), sb(tag + "_var", [P, NB], F32)
    gap, rstd, shift = sb(tag + "_gap", [P, NB], F32), sb(tag + "_rstd", [P, NB], F32), sb(tag + "_shift", [P, NB], F32)
    s_stats, s_small, s_ln, s_rstd, s_shift = (sem(f"{tag}_{n}") for n in ("stats", "small", "ln", "rstd", "shift"))
    s_dve, s_act, s_out = sem(tag + "_dve"), sem(tag + "_act"), sem(tag + "_out")
    own = PB // 2
    with nc.Block() as block:
        @block.vector
        def _(dve):
            with dve.Fori(0, NT) as j:
                for b in range(PB):
                    nc.vector.bn_stats(at(stats, j * PB + b), at(X, j * PB + b)).then_inc(s_stats, 1)
            dve.wait_ge(s_stats, NB)
            nc.vector.tensor_tensor(mean[:, :], stats[:, :, 1], stats[:, :, 4], ALU.add).then_inc(s_small, 1)
            nc.vector.tensor_tensor(gap[:, :], stats[:, :, 1], stats[:, :, 4], ALU.subtract).then_inc(s_small, 1)
            nc.vector.tensor_tensor(var[:, :], stats[:, :, 2], stats[:, :, 5], ALU.add).then_inc(s_small, 1)
            dve.wait_ge(s_small, 3)
            nc.vector.tensor_scalar(mean[:, :], mean[:, :], 0.5, None, ALU.mult).then_inc(s_small, 1)
            nc.vector.scalar_tensor_tensor(gap[:, :], gap[:, :], 0.25, gap[:, :], ALU.mult, ALU.mult).then_inc(s_small, 1)
            dve.wait_ge(s_small, 5)
            nc.vector.scalar_tensor_tensor(var[:, :], var[:, :], 1.0 / C, gap[:, :], ALU.mult, ALU.add).then_inc(s_small, 1)
            dve.wait_ge(s_rstd, 1)
            nc.vector.scalar_tensor_tensor(shift[:, :], mean[:, :], -1.0, rstd[:, :], ALU.mult, ALU.mult).then_inc(s_shift, 1)
            with dve.Fori(0, NT) as j:
                for b in range(own):
                    x = at(X, j * PB + b)
                    last = nc.vector.tensor_scalar(x, x, mean[:, bass.ds(j * PB + b, 1)], rstd[:, bass.ds(j * PB + b, 1)],
                                                   ALU.subtract, ALU.mult)
                last.then_inc(s_dve, 1)

        @block.scalar
        def _(act):
            nc.scalar.preload_act_table_set(EXP_LN)
            act.wait_ge(s_small, 6)
            nc.scalar.activation(rstd[:, :], var[:, :], ACT.Ln, bias=eps_col[:, :]).then_inc(s_ln, 1)
            act.wait_ge(s_ln, 1)
            nc.scalar.activation(rstd[:, :], rstd[:, :], ACT.Exp, scale=-0.5).then_inc(s_rstd, 1)
            act.wait_ge(s_shift, 1)
            with act.Fori(0, NT) as j:
                for b in range(own, PB):
                    x = at(X, j * PB + b)
                    last = nc.scalar.activation(x, x, ACT.Identity, bias=shift[:, bass.ds(j * PB + b, 1)],
                                                scale=rstd[:, bass.ds(j * PB + b, 1)])
                last.then_inc(s_act, 1)

        if out is not None:
            @block.sync
            def _(sp):
                dst = out.rearrange("(n p) c -> p n c", p=P)
                with sp.Fori(0, NT) as j:
                    sp.wait_ge(s_dve, j + 1)
                    sp.wait_ge(s_act, j + 1)
                    sp.dma_start(dst[:, bass.ds(j * PB, PB), :], X[:, bass.ds(j * PB, PB), :]).then_inc(s_out, 16)
                sp.wait_ge(s_out, 16 * NT)


def cross_attention(nc, a, X, ident, sem, sb, part):
    qc = sb("qc", [P, 2, TOK], BF16)
    kh = sb("kh", [P, 2, TOK], BF16)
    KV = sb("KV", [P, NB, P], F32)
    WQ = sb("WQ", [P, 2, HP, 3, P], BF16)
    WB = sb("WB", [P, 2, HP, C], BF16)
    mask = sb("mask", [P, B, T], F32)
    tabs = sb("tabs", [P, 4, T], F32)
    s_setup = sem("x_setup")

    with ExitStack() as own:
        def tmp(name, shape, dt=F32):
            return own.enter_context(nc.sbuf_tensor(name, shape, dt))

        def ps(name, n=TILE):
            return own.enter_context(nc.psum_tensor(name, [P, n], F32))

        ctxf, ctxT = tmp("ctxf", [P, CC, TILE]), tmp("ctxT", [P, 2, CC, TILE], BF16)
        x1T = tmp("x1T", [P, 2, CC, TILE], BF16)
        dqf, dq = tmp("dqf", [P, CC, QC]), tmp("dq", [P, 2, CC, QC], BF16)
        kvf, kvw = tmp("kvf", [P, CC, KVC]), tmp("kvw", [P, 2, CC, KVC], BF16)
        wkr = tmp("wkr", [KVC, 2 * R])
        uqT, ukT, uvT = tmp("uqT", [P, H, QC]), tmp("ukT", [P, H, KVC]), tmp("uvT", [P, H, KVC])
        wo = tmp("wo", [P, H, C])
        qr, qrs = tmp("qr", [QC, H * R]), tmp("qrs", [QC, H * R])
        kf, ksw = tmp("kf", [P, TILE]), tmp("ksw", [P, TILE])
        seg, segf, keys = tmp("seg", [P, B], I32), tmp("segf", [P, B]), tmp("keys", [P, T])
        s_ld, s_ctx = sem("x_loads"), sem("x_ctx")
        n_loads = 16

        with ExitStack() as fold:
            AP_ = fold.enter_context(nc.psum_tensor("foldA", [P, H * KVC], F32))
            BP_ = fold.enter_context(nc.psum_tensor("foldB", [P, HP * C], F32))
            s_A, s_B, s_whi, s_wlo, s_z, s_m = (sem("x_" + n) for n in ("A", "B", "whi", "wlo", "zero", "mask"))
            foldA = AP_[0:QC, :].rearrange("p (g i k) -> p g i k", g=HP, i=2)
            foldB = BP_[:, :].rearrange("p (g c) -> p g c", g=HP)
            qr_v = qr[:, :].rearrange("p (g i k) -> p g i k", g=HP, i=2)
            qrs_v = qrs[:, :].rearrange("p (g i k) -> p g i k", g=HP, i=2)
            splits = [(dqf[:, :, :], lambda k: dq[:, k]), (kvf[:, :, :], lambda k: kvw[:, k]),
                      (qr_v, lambda k: WQ[0:QC, k, :, 0:2, KVC:P]),
                      (qrs_v[:, :, 1], lambda k: WQ[0:QC, k, :, 2, 0:R]),
                      (qrs_v[:, :, 0], lambda k: WQ[0:QC, k, :, 2, R:P]),
                      (foldA, lambda k: WQ[0:QC, k, :, 0:2, 0:KVC]),
                      (foldB, lambda k: WB[:, k])]
            with nc.Block() as block:
                @block.sync
                def _(sp):
                    loads = [(dqf[:, :, :], a["L0_xattn_W_dq"].rearrange("(c p) n -> p c n", p=P)),
                             (kvf[:, :, :], a["L0_xattn_W_kvc"].rearrange("(c p) n -> p c n", p=P)),
                             (wkr[:, :], a["wkr"]),
                             (uqT[:, :, :], a["uqT"].rearrange("(h p) n -> p h n", p=P)),
                             (ukT[:, :, :], a["ukT"].rearrange("(h p) n -> p h n", p=P)),
                             (uvT[:, :, :], a["uvT"].rearrange("(h p) n -> p h n", p=P)),
                             (wo[:, :, :], a["L0_xattn_W_o"].rearrange("(h p) n -> p h n", p=P)),
                             (qr[:, :], a["L0_xattn_W_qr"]), (qrs[:, :], a["qrs"]),
                             (tabs[:, :, :], a["rope"].rearrange("p (k t) -> p k t", k=4)),
                             (keys[:, :], a["keys"]),
                             (seg[0:T, :], a["segT"]), (seg[T:P, :], a["segT"])]
                    for dst, src in loads:
                        sp.dma_start(dst, src).then_inc(s_ld, 16)
                    assert len(loads) == 13

                @block.gpsimd
                def _(pool):
                    nc.gpsimd.memset(WQ[:, :, :, :, :], 0.0).then_inc(s_z, 1)
                    nc.gpsimd.memset(qc[:, :, :], 0.0)
                    nc.gpsimd.memset(KV[:, :, :], 0.0)

                @block.tensor
                def _(pe):
                    pe.wait_ge(s_ld, 13 * 16)
                    for h in range(H):
                        last = nc.tensor.matmul(AP_[0:QC, h * KVC:(h + 1) * KVC], uqT[:, h, :], ukT[:, h, :], start=True, stop=True)
                    last.then_inc(s_A, 1)
                    for h in range(H):
                        o = KVC * (h % 2)
                        last = nc.tensor.matmul(BP_[o:o + KVC, (h // 2) * C:(h // 2 + 1) * C], uvT[:, h, :], wo[:, h, :], start=True, stop=True)
                    last.then_inc(s_B, 1)

                @block.scalar
                def _(act):
                    act.wait_ge(s_ld, 13 * 16)
                    act.wait_ge(s_z, 1)
                    for i, (src, dst) in enumerate(splits):
                        if src is foldA:
                            act.wait_ge(s_A, 1)
                        if src is foldB:
                            act.wait_ge(s_B, 1)
                        nc.scalar.activation(dst(0), src, ACT.Copy).then_inc(s_whi, 1)

                @block.vector
                def _(dve):
                    dve.wait_ge(s_ld, 13 * 16)
                    nc.vector.tensor_copy(segf[:, :], seg[:, :]).then_inc(s_m, 1)
                    dve.wait_ge(s_m, 1)
                    nc.vector.tensor_tensor(mask[:, :, :], segf[:, :].unsqueeze(2).to_broadcast([P, B, T]),
                                            keys[:, :].unsqueeze(1).to_broadcast([P, B, T]), ALU.subtract).then_inc(s_m, 1)
                    dve.wait_ge(s_m, 2)
                    nc.vector.tensor_tensor(mask[:, :, :], mask[:, :, :], mask[:, :, :], ALU.mult).then_inc(s_m, 1)
                    dve.wait_ge(s_m, 3)
                    nc.vector.tensor_scalar(mask[:, :, :], mask[:, :, :], (LOOKBACK / 2) ** 2, NEG, ALU.is_gt, ALU.mult).then_inc(s_m, 1)
                    for i, (src, dst) in enumerate(splits):
                        dve.wait_ge(s_whi, i + 1)
                        nc.vector.tensor_tensor(dst(1), src, dst(0), ALU.subtract).then_inc(s_wlo, 1)

        kvP, krP, ksP, tkP, qcP = ps("kvP"), ps("krP"), ps("ksP"), ps("tkP"), ps("qcP")
        xtP = ps("xtP", CC * TILE)
        n_ = ("chi", "clo", "kv", "kf", "kr", "krr", "kss", "kf2", "khi", "klo", "tk", "tke", "xt", "xhi", "xlo", "qc", "qhi", "qlo", "krs")
        t_ = {n: sem("xp_" + n) for n in n_}
        with nc.Block() as block:
            @block.sync
            def _(sp):
                src = a["ctxT"].rearrange("(c p) t -> p c t", p=P)
                for j in range(NT):
                    if j:
                        sp.wait_ge(t_["clo"], j)
                    sp.dma_start(ctxf[:, :, :], src[:, :, j * TILE:(j + 1) * TILE]).then_inc(s_ctx, 16)

            @block.tensor
            def _(pe):
                for j in range(NT):
                    for c in range(CC):
                        for b in range(PB):
                            if c == 0 and b == 0 and j:
                                pe.wait_ge(t_["xlo"], j)
                            last = nc.tensor.transpose(xtP[:, c * TILE + b * P:c * TILE + (b + 1) * P],
                                                       X[:, j * PB + b, c * P:(c + 1) * P], ident[:, :])
                    last.then_inc(t_["xt"], 1)
                    pe.wait_ge(t_["clo"], j + 1)
                    if j:
                        pe.wait_ge(t_["kf"], j)
                    for c in range(CC):
                        for i, (u, z) in enumerate(PASSES):
                            last = nc.tensor.matmul(kvP[0:KVC, :], kvw[:, u, c, :], ctxT[:, z, c, :],
                                                    start=(c == 0 and i == 0), stop=(c == CC - 1 and i == 2))
                    last.then_inc(t_["kv"], 1)
                    if j:
                        pe.wait_ge(t_["tke"], j)
                    for b in range(PB):
                        for c in range(CC):
                            for i, (u, z) in enumerate(PASSES):
                                last = nc.tensor.matmul(tkP[:, b * KVC:(b + 1) * KVC], ctxT[:, u, c, b * P:(b + 1) * P], kvw[:, z, c, :],
                                                        start=(c == 0 and i == 0), stop=(c == CC - 1 and i == 2))
                    last.then_inc(t_["tk"], 1)
                    pe.wait_ge(t_["xlo"], j + 1)
                    if j:
                        pe.wait_ge(t_["qlo"], j)
                    for c in range(CC):
                        for i, (u, z) in enumerate(PASSES):
                            last = nc.tensor.matmul(qcP[0:QC, :], dq[:, u, c, :], x1T[:, z, c, :],
                                                    start=(c == 0 and i == 0), stop=(c == CC - 1 and i == 2))
                    last.then_inc(t_["qc"], 1)
                    pe.wait_ge(t_["kf"], j + 1)
                    if j:
                        pe.wait_ge(t_["kss"], j)
                    nc.tensor.matmul(krP[R:P, :], wkr[:, 0:R], kf[0:KVC, :], start=True, stop=True)
                    nc.tensor.matmul(ksP[R:P, :], wkr[:, R:2 * R], kf[0:KVC, :], start=True, stop=True).then_inc(t_["kr"], 1)

            @block.scalar
            def _(act):
                for j in range(NT):
                    tok = slice(j * TILE, (j + 1) * TILE)
                    act.wait_ge(s_ctx, 16 * (j + 1))
                    if j:
                        act.wait_ge(t_["tk"], j)
                    nc.scalar.activation(ctxT[:, 0], ctxf[:, :, :], ACT.Copy).then_inc(t_["chi"], 1)
                    act.wait_ge(t_["xt"], j + 1)
                    if j:
                        act.wait_ge(t_["qc"], j)
                    nc.scalar.activation(x1T[:, 0], xtP[:, :].rearrange("p (c t) -> p c t", c=CC), ACT.Copy).then_inc(t_["xhi"], 1)
                    act.wait_ge(t_["kv"], j + 1)
                    if j:
                        act.wait_ge(t_["klo"], j)
                    nc.scalar.activation(kf[0:KVC, :], kvP[0:KVC, :], ACT.Copy).then_inc(t_["kf"], 1)
                    act.wait_ge(t_["tk"], j + 1)
                    tk = tkP[:, 0:PB * KVC].rearrange("p (b k) -> p b k", b=PB)
                    nc.scalar.activation(KV[0:T, j * PB:(j + 1) * PB, 0:KVC], tk[0:T], ACT.Copy)
                    nc.scalar.activation(KV[T:P, j * PB:(j + 1) * PB, KVC:P], tk[T:P], ACT.Copy).then_inc(t_["tke"], 1)
                    act.wait_ge(t_["qc"], j + 1)
                    nc.scalar.activation(qc[0:QC, 0, tok], qcP[0:QC, :], ACT.Copy).then_inc(t_["qhi"], 1)
                    act.wait_ge(t_["kf2"], j + 1)
                    nc.scalar.activation(kh[:, 0, tok], kf[:, :], ACT.Copy).then_inc(t_["khi"], 1)

            @block.vector
            def _(dve):
                def over_batches(k):
                    return tabs[R:P, k, :].unsqueeze(1).to_broadcast([R, BT, T])

                for j in range(NT):
                    tok = slice(j * TILE, (j + 1) * TILE)
                    dve.wait_ge(t_["chi"], j + 1)
                    nc.vector.tensor_tensor(ctxT[:, 1], ctxf[:, :, :], ctxT[:, 0], ALU.subtract).then_inc(t_["clo"], 1)
                    dve.wait_ge(t_["xhi"], j + 1)
                    nc.vector.tensor_tensor(x1T[:, 1], xtP[:, :].rearrange("p (c t) -> p c t", c=CC), x1T[:, 0], ALU.subtract).then_inc(t_["xlo"], 1)
                    dve.wait_ge(t_["qhi"], j + 1)
                    nc.vector.tensor_tensor(qc[0:QC, 1, tok], qcP[0:QC, :], qc[0:QC, 0, tok], ALU.subtract).then_inc(t_["qlo"], 1)
                    dve.wait_ge(t_["kr"], j + 1)
                    nc.vector.tensor_tensor(kf[R:P, :].rearrange("p (b t) -> p b t", t=T), krP[R:P, :].rearrange("p (b t) -> p b t", t=T),
                                            over_batches(2), ALU.mult).then_inc(t_["krr"], 1)
                    nc.vector.tensor_tensor(ksw[R:P, :].rearrange("p (b t) -> p b t", t=T), ksP[R:P, :].rearrange("p (b t) -> p b t", t=T),
                                            over_batches(3), ALU.mult).then_inc(t_["kss"], 1)
                    dve.wait_ge(t_["kss"], j + 1)
                    nc.vector.tensor_tensor(kf[R:P, :], kf[R:P, :], ksw[R:P, :], ALU.add).then_inc(t_["kf2"], 1)
                    dve.wait_ge(t_["khi"], j + 1)
                    nc.vector.tensor_tensor(kh[:, 1, tok], kf[:, :], kh[:, 0, tok], ALU.subtract).then_inc(t_["klo"], 1)

    qh = sb("qh", [P, 2, BT, 2, T], F32)
    qhl = sb("qhl", [P, 2, BT * 2 * T], BF16)
    turn = sb("turn", [P, 2, BT, T], F32)
    scores = sb("x_scores", [P, BT, T], F32)
    probs = sb("x_probs", [P, BT, T], F32)
    probsT = sb("x_probsT", [P, TILE], F32)
    ntop, total, inv = sb("x_ntop", [P, BT], F32), sb("x_total", [P, BT], F32), sb("x_inv", [P, BT], F32)
    oT = sb("oT", [P, TILE], F32)
    oTl = sb("oTl", [P, TILE], BF16)

    def ps(name, n=TILE):
        return part.enter_context(nc.psum_tensor(name, [P, n], F32))

    qP = [ps("xq0"), ps("xq1"), ps("xq2")]
    sP, ptP, oP = ps("xsP"), ps("xptP"), ps("xoP")
    projP = ps("xprojP", PB * C)
    s_q, s_s, s_pt, s_o, s_proj = (sem("c_" + n) for n in ("q", "s", "pt", "o", "proj"))
    s_rot, s_qh, s_ql, s_bias, s_top, s_exp, s_inv, s_norm = (sem("c_" + n) for n in ("rot", "qh", "ql", "bias", "top", "exp", "inv", "norm"))
    s_pte, s_oa, s_ov, s_ol, s_acc = (sem("c_" + n) for n in ("pte", "oa", "ov", "ol", "acc"))

    def out_parts(src_rows):
        par = src_rows // KVC
        o4 = oP[:, :].rearrange("p (b i t) -> p b i t", b=PB, i=2)
        d4 = oT[:, :].rearrange("p (b q t) -> p b q t", b=PB, q=2)
        return [(d4[i * KVC:(i + 1) * KVC, :, par, :], o4[src_rows:src_rows + KVC, :, i, :]) for i in range(2)]

    with nc.Block() as block:
        @block.tensor
        def _(pe):
            def slot(g, j, n, has):
                if has(0):
                    wait(pe, s_rot, n)
                    for k in range(3):
                        for i, (u, z) in enumerate(PASSES):
                            last = nc.tensor.matmul(qP[k][:, :], at(WQ[:, u, :, k], g), qc[:, z, j * TILE:(j + 1) * TILE],
                                                    start=(i == 0), stop=(i == 2))
                        last.then_inc(s_q, 1)
                if has(1):
                    wait(pe, s_ql, n)
                    wait(pe, s_bias, n - 1)
                    jj, s = (j - 1) % NT, (j - 1) % 2
                    flat = qh[:, s].rearrange("p b i t -> p (b i t)")
                    for b in range(BT):
                        key = slice(jj * TILE + b * T, jj * TILE + (b + 1) * T)
                        for i, (u, z) in enumerate(PASSES):
                            q_part = flat[:, b * P:(b + 1) * P].bitcast(BF16)[:, 1::2] if u == 0 else qhl[:, s, b * P:(b + 1) * P]
                            last = nc.tensor.matmul(sP[:, b * T:(b + 1) * T], q_part, kh[:, z, key], start=(i == 0), stop=(i == 2))
                    last.then_inc(s_s, 1)
                if has(2):
                    wait(pe, s_norm, n - 1)
                    wait(pe, s_pte, n - 2)
                    for b in range(PB):
                        last = nc.tensor.transpose(ptP[:, b * P:(b + 1) * P], probs[:, 2 * b:2 * b + 2, :].rearrange("p b s -> p (b s)"), ident[:, :])
                    last.then_inc(s_pt, 1)
                if has(3):
                    wait(pe, s_ol, n - 2)
                    wait(pe, s_acc, n - 3)
                    wb = [at(WB[:, z], g if j >= 3 else g - 1) for z in range(2)]
                    for b in range(PB):
                        for i, (u, z) in enumerate(PASSES):
                            o_part = high(oT, slice(None), b * P, (b + 1) * P) if u == 0 else oTl[:, b * P:(b + 1) * P]
                            last = nc.tensor.matmul(projP[:, b * C:(b + 1) * C], o_part, wb[z], start=(i == 0), stop=(i == 2))
                    last.then_inc(s_proj, 1)
                if has(2):
                    wait(pe, s_pte, n - 1)
                    wait(pe, s_oa, n - 2)
                    wait(pe, s_ov, n - 2)
                    jj = (j - 2) % NT
                    for b in range(PB):
                        last = nc.tensor.matmul(oP[:, b * P:(b + 1) * P], KV[:, jj * PB + b, :], probsT[:, b * P:(b + 1) * P], start=True, stop=True)
                    last.then_inc(s_o, 1)

            slots(pe, slot, HP)

        @block.scalar
        def _(act):
            def slot(g, j, n, has):
                if has(2):
                    wait(act, s_pt, n - 1)
                    wait(act, s_o, n - 2)
                    nc.scalar.activation(probsT[:, :], ptP[:, :], ACT.Copy).then_inc(s_pte, 1)
                if has(1):
                    wait(act, s_top, n)
                    wait(act, s_inv, n - 1)
                    wait(act, s_pt, n - 1)
                    for b in range(BT):
                        last = nc.scalar.activation(probs[:, b, :], scores[:, b, :], ACT.Exp, bias=ntop[:, b:b + 1], accum_out=total[:, b:b + 1])
                    last.then_inc(s_exp, 1)
                if has(2):
                    wait(act, s_o, n - 1)
                    for dst, src in out_parts(0):
                        last = nc.scalar.activation(dst, src, ACT.Copy)
                    last.then_inc(s_oa, 1)

            nc.scalar.preload_act_table_set(EXP_LN)
            slots(act, slot, HP)

        @block.vector
        def _(dve):
            def slot(g, j, n, has):
                s = j % 2
                if has(2):
                    wait(dve, s_exp, n - 1)
                    nc.vector.reciprocal(inv[:, :], total[:, :]).then_inc(s_inv, 1)
                if has(0):
                    def cut(ap):
                        return ap.rearrange("p (b t) -> p b t", b=BT)

                    def tab(k, lo, hi):
                        return tabs[lo:hi, k, :].unsqueeze(1).to_broadcast([hi - lo, BT, T])

                    for i in range(2):
                        wait(dve, s_q, 3 * n + i + 1)
                        if i == 0:
                            wait(dve, s_s, n - 1)
                        nc.vector.tensor_tensor(qh[:, s, :, i, :], cut(qP[i][:, :]), tab(0, 0, P), ALU.mult)
                    wait(dve, s_q, 3 * n + 3)
                    wait(dve, s_qh, n)
                    nc.vector.tensor_tensor(turn[R:P, 0], cut(qP[2][R:P, :]), tab(1, R, P), ALU.mult)
                    nc.vector.tensor_tensor(turn[R:P, 1], cut(qP[2][0:R, :]), tab(1, 0, R), ALU.mult).then_inc(s_rot, 1)
                    wait(dve, s_rot, n + 1)
                    rope = qh[R:P, s].rearrange("p b i t -> p i b t")
                    nc.vector.tensor_tensor(rope, rope, turn[R:P, :, :, :], ALU.add).then_inc(s_qh, 1)
                if has(1):
                    jj = (j - 1) % NT
                    wait(dve, s_s, n)
                    nc.vector.tensor_tensor(scores[:, :, :], sP[:, :].rearrange("p (b s) -> p b s", b=BT), mask[:, jj * BT:(jj + 1) * BT, :], ALU.add).then_inc(s_bias, 1)
                    wait(dve, s_bias, n)
                    nc.vector.tensor_reduce(ntop[:, :], scores[:, :, :], AX, ALU.max, negate=True).then_inc(s_top, 1)
                if has(3):
                    acc = X[:, ((j - 3) % NT) * PB:((j - 3) % NT + 1) * PB, :]
                    wait(dve, s_proj, n - 2)
                    wait(dve, s_acc, n - 3)
                    nc.vector.tensor_tensor(acc, projP[:, :].rearrange("p (b c) -> p b c", b=PB), acc, ALU.add).then_inc(s_acc, 1)
                if has(2):
                    wait(dve, s_o, n - 1)
                    for dst, src in out_parts(KVC):
                        last = nc.vector.tensor_copy(dst, src)
                    last.then_inc(s_ov, 1)

            slots(dve, slot, HP)

        @block.gpsimd
        def _(pool):
            def slot(g, j, n, has):
                if has(2):
                    wait(pool, s_inv, n - 1)
                    nc.gpsimd.tensor_tensor(probs[:, :, :], probs[:, :, :], inv[:, :].unsqueeze(2).to_broadcast([P, BT, T]), ALU.mult).then_inc(s_norm, 1)
                if has(3):
                    wait(pool, s_oa, n - 2)
                    wait(pool, s_ov, n - 2)
                    wait(pool, s_proj, n - 3)
                    nc.gpsimd.tensor_tensor(oTl[:, :], oT[:, :], high(oT, slice(None), 0, TILE), ALU.subtract).then_inc(s_ol, 1)
                if has(0):
                    s = j % 2
                    wait(pool, s_qh, n + 1)
                    wait(pool, s_s, n - 1)
                    flat = qh[:, s].rearrange("p b i t -> p (b i t)")
                    nc.gpsimd.tensor_tensor(qhl[:, s, :], flat, flat.bitcast(BF16)[:, 1::2], ALU.subtract).then_inc(s_ql, 1)

            slots(pool, slot, HP)


def feed_forward(nc, a, X, ident, sem, sb, part):
    wg, wu, wd = sb("wg", [P, CC, DFF], BF16), sb("wu", [P, CC, DFF], BF16), sb("wd", [P, FC, C], BF16)
    xqT = sb("xqT", [P, CC, TOK], BF16)
    wsc = sb("wsc", [P, 3], F32)
    xsc = sb("xsc", [P, NB], F32)
    gsc, usc = sb("gsc", [P, NB], F32), sb("usc", [P, NB], F32)
    identb = sb("identb", [P, P], BF16)
    magic = sb("magic", [P, 1], F32)

    with ExitStack() as own:
        def tmp(name, shape, dt=F32):
            return own.enter_context(nc.sbuf_tensor(name, shape, dt))

        wf = [tmp("wgf", [P, CC, DFF]), tmp("wuf", [P, CC, DFF]), tmp("wdf", [P, FC, C])]
        wq = [wg, wu, wd]
        ones = tmp("onesf", [P, P])
        sums = tmp("wsums", [P, 3])
        winv, xinv = tmp("winv", [P, 3]), tmp("xinv", [P, NB])
        xs, xq = tmp("xs", [P, NB, C]), tmp("xq", [P, NB, C], BF16)
        sumP = own.enter_context(nc.psum_tensor("wsumP", [P, TILE], F32))
        tP = [own.enter_context(nc.psum_tensor(f"xqP{i}", [P, CC * TILE], BF16)) for i in range(2)]
        s_ld, s_d, s_ones, s_sum, s_sumP, s_t, s_te, s_xq, s_id = (sem("fp_" + n) for n in ("ld", "dve", "ones", "sum", "sumP", "t", "te", "xq", "id"))
        with nc.Block() as block:
            @block.sync
            def _(sp):
                sp.dma_start(wf[0][:, :, :], a["wgT"].rearrange("(c p) n -> p c n", p=P)).then_inc(s_ld, 16)
                sp.dma_start(wf[1][:, :, :], a["wuT"].rearrange("(c p) n -> p c n", p=P)).then_inc(s_ld, 16)
                sp.dma_start(wf[2][:, :, :], a["wdT"].rearrange("(c p) n -> p c n", p=P)).then_inc(s_ld, 16)

            @block.vector
            def _(dve):
                done = [0]

                def then(ins):
                    done[0] += 1
                    ins.then_inc(s_d, 1)
                    dve.wait_ge(s_d, done[0])

                nc.vector.memset(ones[:, :], 1.0).then_inc(s_ones, 1)
                nc.vector.memset(magic[:, :], MAGIC)
                nc.vector.tensor_copy(identb[:, :], ident[:, :]).then_inc(s_id, 1)
                then(nc.vector.tensor_reduce(xsc[:, :], X[:, :, :], AX, ALU.max, apply_absolute_value=True))
                then(nc.vector.tensor_scalar(xsc[:, :], xsc[:, :], EPS, 1.0 / 127.0, ALU.max, ALU.mult))
                then(nc.vector.reciprocal(xinv[:, :], xsc[:, :]))
                then(nc.vector.tensor_tensor(xs[:, :, :], X[:, :, :], xinv[:, :].unsqueeze(2).to_broadcast([P, NB, C]), ALU.mult))
                then(nc.vector.tensor_scalar(xs[:, :, :], xs[:, :, :], MAGIC, None, ALU.add))
                nc.vector.tensor_scalar(xq[:, :, :], xs[:, :, :], MAGIC, None, ALU.subtract).then_inc(s_xq, 1)
                dve.wait_ge(s_ld, 3 * 16)
                for k in range(3):
                    nc.vector.tensor_reduce(sums[:, k:k + 1], wf[k][:, :, :].rearrange("p a b -> p (a b)"), AX, ALU.add,
                                            apply_absolute_value=True).then_inc(s_sum, 1)
                dve.wait_ge(s_sumP, 1)
                then(nc.vector.tensor_scalar(wsc[:, :], sumP[:, 0:3], 1.0 / (C * DFF), EPS, ALU.mult, ALU.add))
                then(nc.vector.reciprocal(winv[:, :], wsc[:, :]))
                for k in range(3):
                    then(nc.vector.tensor_scalar(wf[k][:, :, :], wf[k][:, :, :], winv[:, k:k + 1], MAGIC, ALU.mult, ALU.add))
                    then(nc.vector.tensor_scalar(wf[k][:, :, :], wf[k][:, :, :], MAGIC, 1.0, ALU.subtract, ALU.min))
                    nc.vector.tensor_scalar(wq[k][:, :, :], wf[k][:, :, :], -1.0, None, ALU.max)
                nc.vector.tensor_scalar(gsc[:, :], xsc[:, :], wsc[:, 0:1], None, ALU.mult)
                nc.vector.tensor_scalar(usc[:, :], xsc[:, :], wsc[:, 1:2], None, ALU.mult)

            @block.tensor
            def _(pe):
                pe.wait_ge(s_xq, 1)
                pe.wait_ge(s_id, 1)
                for j in range(NT):
                    if j >= 2:
                        pe.wait_ge(s_te, j - 1)
                    for c in range(CC):
                        for b in range(PB):
                            last = nc.tensor.transpose(tP[j % 2][:, c * TILE + b * P:c * TILE + (b + 1) * P],
                                                       xq[:, j * PB + b, c * P:(c + 1) * P], identb[:, :])
                    last.then_inc(s_t, 1)
                pe.wait_ge(s_sum, 3)
                pe.wait_ge(s_ones, 1)
                nc.tensor.matmul(sumP[:, 0:3], ones[:, :], sums[:, :], start=True, stop=True).then_inc(s_sumP, 1)

            @block.scalar
            def _(act):
                for j in range(NT):
                    act.wait_ge(s_t, j + 1)
                    nc.scalar.activation(xqT[:, :, j * TILE:(j + 1) * TILE], tP[j % 2][:, :].rearrange("p (c t) -> p c t", c=CC), ACT.Copy).then_inc(s_te, 1)

    UN = 4
    sig, hs = sb("sig", [P, 2, DFF], F32), sb("hs", [P, 2, DFF], F32)
    hm = sb("hm", [P, 2, DFF], F32)
    hqT = sb("hqT", [P, 2, DFF], BF16)
    hsc, hinv = sb("hsc", [P, UN], F32), sb("hinv", [P, UN], F32)
    dsc = sb("dsc", [P, UN], F32)
    gP, uP, tP = (part.enter_context(nc.psum_tensor(n, [P, DFF], F32)) for n in ("gP", "uP", "hmP"))
    dP = part.enter_context(nc.psum_tensor("dP", [P, TILE], F32))
    s_g, s_u, s_t, s_dn = (sem("f_" + n) for n in ("g", "u", "t", "dn"))
    s_sig, s_h, s_max, s_sc, s_inv, s_dsc, s_hm, s_te, s_y = (sem("f_" + n) for n in ("sig", "h", "max", "sc", "inv", "dsc", "hm", "te", "y"))

    def column(tile, n):
        return tile[:, n:n + 1] if isinstance(n, int) else tile[:, bass.ds(n, 1)]

    with nc.Block() as block:
        @block.tensor
        def _(pe):
            def slot(g, j, n, has):
                if has(0):
                    for w, dst, free, ready in ((wg, gP, s_sig, s_g), (wu, uP, s_h, s_u)):
                        wait(pe, free, n)
                        for f in range(DFF // TILE):
                            for c in range(CC):
                                x = xqT[:, c, n * P:(n + 1) * P] if isinstance(n, int) else xqT[:, c, bass.ds(n * P, P)]
                                last = nc.tensor.matmul(dst[:, f * TILE:(f + 1) * TILE], x, w[:, c, f * TILE:(f + 1) * TILE],
                                                        start=(c == 0), stop=(c == CC - 1))
                        last.then_inc(ready, 1)
                if has(2):
                    wait(pe, s_hm, n - 1)
                    wait(pe, s_te, n - 2)
                    for f in range(FC):
                        last = nc.tensor.transpose(tP[:, f * P:(f + 1) * P], hm[:, j % 2, f * P:(f + 1) * P], ident[:, :])
                    last.then_inc(s_t, 1)
                if has(3):
                    wait(pe, s_te, n - 2)
                    wait(pe, s_y, n - 3)
                    for f in range(FC):
                        last = nc.tensor.matmul(dP[:, 0:C], hqT[:, (j - 3) % 2, f * P:(f + 1) * P], wd[:, f, :], start=(f == 0), stop=(f == FC - 1))
                    last.then_inc(s_dn, 1)

            slots(pe, slot, NB // UN, UN)

        @block.scalar
        def _(act):
            def slot(g, j, n, has):
                if has(0):
                    wait(act, s_g, n + 1)
                    wait(act, s_h, n - 1)
                    nc.scalar.activation(sig[:, j % 2, :], gP[:, :], ACT.Sigmoid, scale=column(gsc, n)).then_inc(s_sig, 1)
                if has(1):
                    s, jj = (j - 1) % 2, (j - 1) % UN
                    wait(act, s_inv, n)
                    wait(act, s_t, n - 2)
                    nc.scalar.activation(hm[:, s, :], hs[:, s, :], ACT.Identity, bias=magic[:, :], scale=hinv[:, jj:jj + 1]).then_inc(s_hm, 1)
                if has(2):
                    wait(act, s_t, n - 1)
                    wait(act, s_dn, n - 3)
                    nc.scalar.activation(hqT[:, j % 2, :], tP[:, :], ACT.Copy, bias=-MAGIC).then_inc(s_te, 1)

            slots(act, slot, NB // UN, UN)

        @block.vector
        def _(dve):
            def slot(g, j, n, has):
                if has(0):
                    wait(dve, s_sig, n + 1)
                    wait(dve, s_u, n + 1)
                    wait(dve, s_hm, n - 1)
                    nc.vector.scalar_tensor_tensor(hs[:, j % 2, :], uP[:, :], column(usc, n), sig[:, j % 2, :],
                                                   ALU.mult, ALU.mult).then_inc(s_h, 1)
                    wait(dve, s_h, n + 1)
                    nc.vector.tensor_reduce(hsc[:, j:j + 1], hs[:, j % 2, :], AX, ALU.max, apply_absolute_value=True).then_inc(s_max, 1)
                    wait(dve, s_max, n + 1)
                    nc.vector.tensor_scalar(hsc[:, j:j + 1], hsc[:, j:j + 1], EPS, 1.0 / 127.0, ALU.max, ALU.mult).then_inc(s_sc, 1)
                    wait(dve, s_sc, n + 1)
                    nc.vector.reciprocal(hinv[:, j:j + 1], hsc[:, j:j + 1]).then_inc(s_inv, 1)
                    nc.vector.tensor_scalar(dsc[:, j:j + 1], hsc[:, j:j + 1], wsc[:, 2:3], None, ALU.mult).then_inc(s_dsc, 1)
                if has(3):
                    jj = (j - 3) % UN
                    wait(dve, s_dn, n - 2)
                    wait(dve, s_dsc, n - 2)
                    x = at(X, n - 3)
                    nc.vector.scalar_tensor_tensor(x, dP[:, 0:C], dsc[:, jj:jj + 1], x, ALU.mult, ALU.add).then_inc(s_y, 1)

            slots(dve, slot, NB // UN, UN)


def constants():
    import numpy as np

    t = np.arange(P)
    same = (t[:, None] // T) == (t[None, :] // T)
    dist = (t[:, None] % T) - (t[None, :] % T)
    slopes = np.array([2.0 ** (-8.0 * (h + 1) / H) for h in range(H)])
    bias = np.where(dist >= 0, -dist[:, None, :].transpose(1, 0, 2) * slopes[:, None, None], NEG)
    bias = np.where(same, bias, NEG).transpose(1, 0, 2).reshape(P, H * P)
    half = R // 2
    freq = 1.0 / 10000.0 ** (np.arange(half) / half)
    ang = (np.arange(T)[:, None] * freq).T
    cos, sin = np.concatenate([np.cos(ang)] * 2), np.concatenate([-np.sin(ang), np.sin(ang)])
    one, scale = np.ones((KVC, T)), 1.0 / np.sqrt(D + R)
    rope = np.concatenate([np.concatenate([one, cos]) * scale, np.concatenate([sin, sin]) * scale,
                           np.concatenate([cos, cos]), np.concatenate([sin, sin])], axis=1)
    keys = np.tile(np.arange(T) + LOOKBACK / 2, (P, 1))
    return {"ident": np.eye(P, dtype=np.float32), "bias": bias.astype(np.float32),
            "rope": rope.astype(np.float32), "keys": keys.astype(np.float32)}


def kernel(**inputs):
    import numpy as np
    import concourse.bacc as bacc
    from concourse.bass_utils import run_bass_kernel_spmd

    nc = bacc.Bacc("TRN2", target_bir_lowering=False, num_devices=1)
    x = np.asarray(inputs["x"])
    arrays = {"x": x.reshape(TOK, C), "xT": x.reshape(TOK, C).T,
              "ctxT": np.asarray(inputs["ctx_2048"]).reshape(TOK, C).T,
              "segT": np.asarray(inputs["itok_BxS_0_1023"]).T}
    for name in ("L0_attn_Wq", "L0_attn_Wk", "L0_attn_Wv", "L0_attn_Wproj", "L0_attn_q_rms_w", "L0_attn_k_rms_w",
                 "L0_attn_subln_w", "L0_xattn_W_dq", "L0_xattn_W_kvc", "L0_xattn_W_o", "L0_xattn_W_qr"):
        arrays[name] = np.asarray(inputs[name])
    swap = np.concatenate([np.arange(R // 2, R), np.arange(R // 2)])
    W_qr, W_kr = np.asarray(inputs["L0_xattn_W_qr"]), np.asarray(inputs["L0_xattn_W_kr"])
    arrays["qrs"] = W_qr.reshape(QC, H, R)[:, :, swap].reshape(QC, H * R)
    arrays["wkr"] = np.concatenate([W_kr, W_kr[:, swap]], axis=1)
    for short, name in (("uqT", "L0_xattn_W_uq"), ("ukT", "L0_xattn_W_uk"), ("uvT", "L0_xattn_W_uv"),
                        ("wgT", "L0_ffn_w_gate"), ("wuT", "L0_ffn_w_up"), ("wdT", "L0_ffn_w_down")):
        arrays[short] = np.asarray(inputs[name]).T
    arrays.update(constants())
    arrays = {n: np.ascontiguousarray(v) for n, v in arrays.items()}
    a = {n: nc.dram_tensor("in_" + n, v.shape, mybir.dt.from_np(v.dtype), kind="ExternalInput").ap() for n, v in arrays.items()}
    out = nc.dram_tensor("out", (TOK, C), F32, kind="ExternalOutput").ap()
    build(nc, a, out)
    r = run_bass_kernel_spmd(nc, [{"in_" + n: v for n, v in arrays.items()}], core_ids=[0])
    return r.results[0]["out"].reshape(B, T, C)
```
